# Optimizing a Trainium2 kernel written in Bass

```python
import numpy as np
import jax
import jax.numpy as jnp

def _softmax(x, axis=-1):
    return jax.nn.softmax(x, axis=axis)

def _gelu(x):
    return jax.nn.gelu(x, approximate=True)

def _silu(x):
    return jax.nn.silu(x)

def _sigmoid(x):
    return jax.nn.sigmoid(x)

def _layernorm(x, axis=-1, eps=1e-05):
    m = jnp.mean(x, axis=axis, keepdims=True)
    v = jnp.var(x, axis=axis, keepdims=True)
    return (x - m) / jnp.sqrt(v + eps)

def _scatter_add(tgt, idx, src, axis=0):
    return tgt.at[idx].add(src)

def _segment_sum(src, seg, n):
    return jax.ops.segment_sum(src, seg, n)
kernel_name = 'mk_gnn_ffn_d1_gnn_r8_5a1e03'

def setup_inputs(seed: int=0):
    np.random.seed(seed)
    _w = jnp.asarray

    def _rec_inputs():
        import jax
        import jax.numpy as jnp
        _gk = jax.random.key(seed)
        x = -0.0003713 + 1 * jax.random.normal(jax.random.fold_in(_gk, 1), (6250, 256), jnp.float32)
        _s = jax.random.randint(jax.random.fold_in(_gk, 2), (100000,), 0, 6250, jnp.int32)
        _d = jax.random.randint(jax.random.fold_in(_gk, 3), (100000,), 0, 6250, jnp.int32)
        _loop = jnp.arange(6250, dtype=jnp.int32)
        src = jnp.concatenate([_s, _d, _loop])
        dst = jnp.concatenate([_d, _s, _loop])
        _o = jnp.argsort(dst, stable=True)
        src = src[_o]
        dst = dst[_o]
        return (x, src, dst)
    x, src, dst = _rec_inputs()

    def _L0_gnn_setup():
        import jax, jax.numpy as jnp
        import numpy as np
        N_NODES = 6250
        N_EDGES = 200000
        H_SIZE = 256
        HEADS = 8
        HEAD_DIM = H_SIZE // HEADS
        NEG_SLOPE = 0.2
        key = jax.random.key(seed)
        k_x, k_e, k_w, k_as, k_ad, k_b = jax.random.split(key, 6)
        x = jax.random.normal(k_x, (N_NODES, H_SIZE), dtype=jnp.float32)
        edge_index = jax.random.randint(k_e, (2, N_EDGES), 0, N_NODES, dtype=jnp.int64)
        scale = 1.0 / np.sqrt(H_SIZE)
        W = jax.random.normal(k_w, (H_SIZE, HEADS, HEAD_DIM), dtype=jnp.float32) * scale
        att_src = jax.random.normal(k_as, (HEADS, HEAD_DIM), dtype=jnp.float32) * scale
        att_dst = jax.random.normal(k_ad, (HEADS, HEAD_DIM), dtype=jnp.float32) * scale
        bias = jnp.zeros((H_SIZE,), dtype=jnp.float32)
        return {'x': x, 'edge_index': edge_index, 'W': W, 'att_src': att_src, 'att_dst': att_dst, 'bias': bias}
    _L0_gnn_all = _L0_gnn_setup()
    _L0_gnn_in = {k: v for k, v in _L0_gnn_all.items() if k in ('W', 'att_src', 'att_dst', 'bias')}
    del _L0_gnn_all

    def _L0_ffn_setup():
        import jax, jax.numpy as jnp
        import numpy as np
        B, S, H, F, E, K = (8, 512, 256, 512, 16, 2)
        EPS = 1e-05
        key = jax.random.key(seed)
        ks = jax.random.split(key, 9)
        sc = 0.02
        return {'x': jax.random.normal(ks[0], (B, S, H), dtype=jnp.float32), 'gate_w': jax.random.normal(ks[1], (H, E), dtype=jnp.float32) * sc, 'gate_b': jnp.zeros((E,), dtype=jnp.float32), 'w1': jax.random.normal(ks[2], (E, H, F), dtype=jnp.float32) * sc, 'b1': jnp.zeros((E, F), dtype=jnp.float32), 'w2': jax.random.normal(ks[3], (E, F, H), dtype=jnp.float32) * sc, 'b2': jnp.zeros((E, H), dtype=jnp.float32), 'gamma': jnp.ones((H,), dtype=jnp.float32), 'beta': jnp.zeros((H,), dtype=jnp.float32)}
    _L0_ffn_all = _L0_ffn_setup()
    _L0_ffn_in = {k: v for k, v in _L0_ffn_all.items() if k in ('gate_w', 'gate_b', 'w1', 'b1', 'w2', 'b2', 'gamma', 'beta')}
    del _L0_ffn_all
    return {'x': x, 'src': src, 'dst': dst, 'L0_gnn_W': _L0_gnn_in['W'], 'L0_gnn_att_src': _L0_gnn_in['att_src'], 'L0_gnn_att_dst': _L0_gnn_in['att_dst'], 'L0_gnn_bias': _L0_gnn_in['bias'], 'L0_ffn_gate_w': _L0_ffn_in['gate_w'], 'L0_ffn_gate_b': _L0_ffn_in['gate_b'], 'L0_ffn_w1': _L0_ffn_in['w1'], 'L0_ffn_b1': _L0_ffn_in['b1'], 'L0_ffn_w2': _L0_ffn_in['w2'], 'L0_ffn_b2': _L0_ffn_in['b2'], 'L0_ffn_gamma': _L0_ffn_in['gamma'], 'L0_ffn_beta': _L0_ffn_in['beta']}

def reference(x, src, dst, L0_gnn_W, L0_gnn_att_src, L0_gnn_att_dst, L0_gnn_bias, L0_ffn_gate_w, L0_ffn_gate_b, L0_ffn_w1, L0_ffn_b1, L0_ffn_w2, L0_ffn_b2, L0_ffn_gamma, L0_ffn_beta):
    import jax
    import jax.numpy as jnp

    def _L0_gnn_ref(x, edge_index, W, att_src, att_dst, bias):
        import jax, jax.numpy as jnp
        import numpy as np
        N_NODES = 6250
        N_EDGES = 200000
        H_SIZE = 256
        HEADS = 8
        HEAD_DIM = H_SIZE // HEADS
        NEG_SLOPE = 0.2
        'GATConv (concat heads) -> relu -> dropout(eval=identity).\n\n            x: [N, F]; edge_index: [2, E] with (src=row0, dst=row1) meaning message j->i.\n            '
        N = x.shape[0]
        h = jnp.einsum('nf,fhd->nhd', x, W)
        a_src = jnp.sum(h * att_src, axis=-1)
        a_dst = jnp.sum(h * att_dst, axis=-1)
        src = edge_index[0]
        dst = edge_index[1]
        e = jax.nn.leaky_relu(a_src[src] + a_dst[dst], NEG_SLOPE)
        e_max = jax.ops.segment_max(e, dst, num_segments=N)
        e_exp = jnp.exp(e - e_max[dst])
        denom = jax.ops.segment_sum(e_exp, dst, num_segments=N)
        alpha = e_exp / (denom[dst] + 1e-16)
        msg = h[src] * alpha[:, :, None]
        out = jax.ops.segment_sum(msg, dst, num_segments=N)
        out = out.reshape(N, -1) + bias
        return jax.nn.relu(out)

    def _L0_ffn_ref(x, gate_w, gate_b, w1, b1, w2, b2, gamma, beta):
        import jax, jax.numpy as jnp
        import numpy as np
        B, S, H, F, E, K = (8, 512, 256, 512, 16, 2)
        EPS = 1e-05
        gate_logits = x @ gate_w + gate_b
        topk_vals, topk_idx = jax.lax.top_k(gate_logits, K)
        topk_w = jax.nn.softmax(topk_vals, axis=-1)
        h = jax.nn.relu(jnp.einsum('bsh,ehf->bsef', x, w1) + b1)
        expert_out = jnp.einsum('bsef,efh->bseh', h, w2) + b2
        sel = jnp.take_along_axis(expert_out, topk_idx[:, :, :, None], axis=2)
        moe = jnp.sum(topk_w[..., None] * sel, axis=2)
        y = x + moe
        mu = jnp.mean(y, axis=-1, keepdims=True)
        var = jnp.var(y, axis=-1, keepdims=True)
        return (y - mu) / jnp.sqrt(var + EPS) * gamma + beta
    edge_index = jnp.stack([src, dst])
    x = x + _L0_gnn_ref(_layernorm(x, axis=-1), edge_index, L0_gnn_W, L0_gnn_att_src, L0_gnn_att_dst, L0_gnn_bias)
    x = x + _L0_ffn_ref(_layernorm(x, axis=-1)[None], L0_ffn_gate_w, L0_ffn_gate_b, L0_ffn_w1, L0_ffn_b1, L0_ffn_w2, L0_ffn_b2, L0_ffn_gamma, L0_ffn_beta)[0]
    return x

_drawn_inputs = setup_inputs


def setup_inputs(seed=0):
    import zlib

    import numpy as np

    out = dict(_drawn_inputs(seed))
    spreads = {'L0_gnn_bias': (0.0, 0.1),
     'L0_ffn_gate_b': (0.0, 0.1),
     'L0_ffn_b1': (0.0, 0.708),
     'L0_ffn_b2': (0.0, 0.1),
     'L0_ffn_gamma': (1.0, 0.2),
     'L0_ffn_beta': (0.0, 0.1)}
    factors = {'L0_gnn_att_dst': 3.736}
    for name, (base, spread) in spreads.items():
        noise = np.random.default_rng([zlib.crc32(name.encode()), seed]).standard_normal(out[name].shape)
        drawn = base * np.exp(spread * noise) if base else spread * noise
        out[name] = jnp.asarray(drawn.astype(out[name].dtype))
    for name, factor in factors.items():
        out[name] = (out[name] * factor).astype(out[name].dtype)
    return out
```

```python
from contextlib import ExitStack

import concourse.bass as bass
from concourse import mybir

ALU = mybir.AluOpType
ACT = mybir.ActivationFunctionType
AX = mybir.AxisListType
F32 = mybir.dt.float32
BF16 = mybir.dt.bfloat16
I32 = mybir.dt.int32
U32 = mybir.dt.uint32

P = 128
N = 6250
E = 206250
D = 256
H = 8
HD = D // H
NB = (N + P - 1) // P
NPAD = NB * P
LAST = N - (NB - 1) * P
EPS = 1e-5
SLOPE = 0.2

TROW = D + H
WCOL = D + 2 * H
RROW = D + H + 4
C_ADST, C_START, C_DEG, C_ID = D, D + H, D + H + 1, D + H + 2

SEG = 454
NSEG = E // SEG
KEYS = P

GS = 4
W = 64
GW = W // GS
EDGE_PAD = SEG + W
NEG = -1.0e30
MASK = -2.0e30

X = 16
F = 512
FC = F // P
DC = D // P
TOP = 2
FB = (TOP * N + X * (P - 1)) // P
ROWS = FB * P
CLEAR = (FB + NB - 1) // NB

B1 = 7
SRING = B1


class Steps:

    def __init__(self, eng, sem, base=0):
        self.eng, self.sem, self.base, self.n = eng, sem, base, 0

    def do(self, ins):
        ins.then_inc(self.sem, 1)
        self.n += 1

    def settle(self):
        after(self.eng, self.sem, self.base + self.n)


def after(eng, sem, value):
    if not isinstance(value, int) or value > 0:
        eng.wait_ge(sem, value)


def peeled(eng, n, body):
    body(0)
    with eng.Fori(1, n) as k:
        body(k)


def alternating(eng, n, body):
    body(0, 0, 0)
    body(1, 1, 0)
    with eng.Fori(1, n // 2) as k:
        body(2 * k, 0, k)
        body(2 * k + 1, 1, k)
    for i in range(n // 2 * 2, n):
        body(i, i % 2, i // 2)


def cycling(eng, n, ring, body):
    for i in range(ring):
        body(i, i, 0)
    with eng.Fori(1, n // ring) as k:
        for i in range(ring):
            body(k * ring + i, i, k)
    for i in range(n // ring * ring, n):
        body(i, i % ring, i // ring)


def gnn_ffn_kernel(nc, x, src, dst, w, att_src, att_dst, bias, gate_w, gate_b, w1, b1, w2, b2, gamma, beta, out):
    src_pad = nc.dram_tensor("src_pad", [E + EDGE_PAD, 1], I32).ap()
    dst_pad = nc.dram_tensor("dst_pad", [E + EDGE_PAD, 1], I32).ap()
    table = nc.dram_tensor("table", [NPAD, TROW], F32).ap()
    records = nc.dram_tensor("records", [NPAD, RROW], F32).ap()
    xy = nc.dram_tensor("xy", [NPAD, 2 * D], F32).ap()
    queue_in = nc.dram_tensor("queue_in", [NB * CLEAR * P, D], F32).ap()
    queue_out = nc.dram_tensor("queue_out", [ROWS, D], F32).ap()

    with ExitStack() as ctx:
        def sb(name, shape, dt=F32):
            return ctx.enter_context(nc.sbuf_tensor(name, shape, dt))

        def sem(name):
            return ctx.enter_context(nc.semaphore(name))

        bank = [ctx.enter_context(nc.psum_tensor(f"bank{i}", [P, 512], F32)) for i in range(8)]

        ident = sb("ident", [P, P])
        upper = sb("upper", [P, P], BF16)
        ones_b = sb("ones_b", [P, P], BF16)
        iota_x = sb("iota_x", [P, X])
        iota_w = sb("iota_w", [P, W])
        eps = sb("eps", [P, 1])
        plan = sb("plan", [1, 4, NB], I32)
        arena = sb("arena", [P, 2 * W * TROW])
        rec = arena[:, 0:NB * RROW].rearrange("p (b r) -> p b r", r=RROW)

        pick = sb("pick", [P, TOP, NB, X])
        share = sb("share", [P, NB, TOP])
        rank = sb("rank", [P, NB, TOP])
        chosen = sb("chosen", [P, X], BF16)
        ids = sb("ids", [P, NB], I32)

        build_graph(nc, ctx, locals())
        attend(nc, ctx, locals())
        experts(nc, ctx, locals())


def build_graph(nc, outer, g):
    x, src, dst, w, att_src, att_dst = (g[k] for k in ("x", "src", "dst", "w", "att_src", "att_dst"))
    src_pad, dst_pad, table, records = (g[k] for k in ("src_pad", "dst_pad", "table", "records"))
    ident, upper, ones_b, iota_x, iota_w, eps, plan, arena, rec, bank = (
        g[k] for k in ("ident", "upper", "ones_b", "iota_x", "iota_w", "eps", "plan", "arena", "rec", "bank"))
    EDGE_ROWS = 250
    at = [NB * RROW]

    with ExitStack() as ctx:
        def sb(name, shape, dt=F32):
            return ctx.enter_context(nc.sbuf_tensor(name, shape, dt))

        def sem(name):
            return ctx.enter_context(nc.semaphore(name))

        def spare(words):
            a = arena[:, at[0]:at[0] + words]
            at[0] += words
            assert at[0] <= 2 * W * TROW
            return a

        upper_f = sb("upper_f", [P, P])
        iota_key = sb("iota_key", [P, KEYS])
        iota_blk = sb("iota_blk", [P, NB])
        node = sb("node", [P, NB])
        next_row = sb("next_row", [P, P])
        wrap_row = sb("wrap_row", [P, P])
        w_sb = sb("w_sb", [P, DC, WCOL])
        att = sb("att", [P, 2, D])
        watt = sb("watt", [P, 2, D])
        stats = sb("stats", [P, NB, 6])
        mean = sb("mean", [P, NB])
        gap = sb("gap", [P, NB])
        spread = sb("spread", [P, NB])
        std = sb("std", [P, NB])
        rstd = sb("rstd", [P, NB])
        xn = spare(B1 * D).rearrange("p (b d) -> p b d", b=B1)
        xnT = spare(2 * D).rearrange("p (b c n) -> p b c n", b=2, c=DC)
        hrow = spare(B1 * TROW).rearrange("p (b r) -> p b r", b=B1)
        tail_i = sb("tail_i", [1, NSEG], I32)
        tail_f = sb("tail_f", [1, NSEG])
        ones_f = sb("ones_f", [1, P])
        full_seg = sb("full_seg", [P, NB])
        seg_at = sb("seg_at", [P, NB], I32)
        seg_row = spare(SRING * SEG).bitcast(I32).rearrange("p (r s) -> p r s", r=SRING)
        junk = spare(2 * SEG).rearrange("p (b s) -> p b s", b=2)
        in_seg = sb("in_seg", [P, NB])
        start = sb("start", [P, NB + 1])
        deg = sb("deg", [P, NB])
        key = sb("key", [P, NB])
        classes = spare(KEYS * NB // 2).bitcast(BF16).rearrange("p (k t) -> p k t", k=KEYS)
        carry = spare(KEYS * NB // 2).bitcast(BF16).rearrange("p (k t) -> p k t", k=KEYS)
        running = spare(KEYS * NB // 2).bitcast(BF16).rearrange("p (k t) -> p k t", k=KEYS)
        count = sb("count", [P, 1])
        count_b = sb("count_b", [P, P])
        upto = sb("upto", [P, 1])
        passed = sb("passed", [P, NB], BF16)
        position = sb("position", [P, NB])
        position_i = sb("position_i", [P, NB], I32)
        deg_max = sb("deg_max", [P, 1])
        deg_top = sb("deg_top", [1, 1])
        k_max = sb("k_max", [1, NB])
        k_hit = sb("k_hit", [1, NB])
        plan_i = sb("plan_i", [1, 4, NB], I32)
        plan_f = sb("plan_f", [1, 3, NB])
        plan_t = sb("plan_t", [1, 3, NB])
        row_one = sb("row_one", [1, NB])
        zrow = sb("zrow", [P, EDGE_PAD], I32)

        x_loaded = sem("x_loaded")
        w_loaded = sem("w_loaded")
        tail_loaded = sem("tail_loaded")
        edges_padded = sem("edges_padded")
        pads_ready = sem("pads_ready")
        pool_made = sem("pool_made")
        vec = sem("vec")
        vec_b = sem("vec_b")
        tail_row_ready = sem("tail_row_ready")
        tail_spread = sem("tail_spread")
        seg_found = sem("seg_found")
        seg_gathered = [sem(f"seg_gathered{i}") for i in range(SRING)]
        seg_counted = sem("seg_counted")
        w_ready = sem("w_ready")
        tile_stats = sem("tile_stats")
        var_ready = sem("var_ready")
        std_ready = sem("std_ready")
        xn_ready = sem("xn_ready")
        xn_turned = sem("xn_turned")
        xnT_ready = sem("xnT_ready")
        projected = sem("projected")
        hrow_ready = sem("hrow_ready")
        adst_ready = sem("adst_ready")
        h_stored = [sem(f"h_stored{j}") for j in range(B1)]
        start_ready = sem("start_ready")
        end_spread = sem("end_spread")
        classes_ready = sem("classes_ready")
        counted = sem("counted")
        count_ready = sem("count_ready")
        upto_ready = sem("upto_ready")
        passed_ready = sem("passed_ready")
        blocks_counted = sem("blocks_counted")
        max_ready = sem("max_ready")
        max_turned = sem("max_turned")
        running_ready = sem("running_ready")
        ranked = sem("ranked")
        rank_read = sem("rank_read")
        position_ready = sem("position_ready")
        records_stored = sem("records_stored")

        ps_turn = [bank[0], bank[1]]
        ps_proj = [bank[2], bank[3]]
        ps_tail = bank[4]
        ps_small = bank[5]
        ps_rank = [bank[6], bank[7]]
        POOL_MADE = 18

        block = ctx.enter_context(nc.Block())

        @block.sync
        def _(sp):
            with nc.allow_non_contiguous_dma(reason="one dst of each segment"):
                tails = dst[0:NSEG * SEG].rearrange("(o j s) -> o j s", o=1, s=SEG)[:, :, SEG - 1:SEG]
                sp.dma_start(tail_i[0:1, :].rearrange("o (j s) -> o j s", s=1), tails).then_inc(tail_loaded, 16)
            for a, b in ((src, src_pad), (dst, dst_pad)):
                sp.dma_start(b[0:E, :].rearrange("(r c) o -> r (c o)", r=EDGE_ROWS),
                             a.rearrange("(r c) -> r c", r=EDGE_ROWS)).then_inc(edges_padded, 16)
            sp.wait_ge(pads_ready, 2)
            sp.dma_start(src_pad[E:E + EDGE_PAD, :].rearrange("(o c) e -> o (c e)", o=1),
                         zrow[0:1, :]).then_inc(edges_padded, 16)
            sp.dma_start(dst_pad[E:E + EDGE_PAD, :].rearrange("(o c) e -> o (c e)", o=1),
                         zrow[32:33, :]).then_inc(edges_padded, 16)
            for c in range(DC):
                sp.dma_start(w_sb[:, c, 0:D], w.rearrange("f h d -> f (h d)")[c * P:(c + 1) * P, :]).then_inc(w_loaded, 16)
            for i, a in enumerate((att_src, att_dst)):
                sp.dma_start(att[:, i, :], a.rearrange("(o h) d -> o (h d)", o=1).partition_broadcast(P)).then_inc(w_loaded, 16)
            sp.wait_ge(pads_ready, 3)
            for k in range(NB // B1):
                n_full = B1 if k < NB // B1 - 1 else B1 - 1
                t0 = k * B1
                sp.dma_start(rec[:, t0:t0 + n_full, 0:D],
                             x[t0 * P:(t0 + n_full) * P, :].rearrange("(t p) d -> p t d", p=P)).then_inc(x_loaded, 16)
            sp.dma_start(rec[0:LAST, NB - 1, 0:D], x[(NB - 1) * P:N, :]).then_inc(x_loaded, 16)
            with nc.sync.Fori(0, NB // B1) as k:
                for j in range(B1):
                    t = k * B1 + j
                    sp.wait_ge(hrow_ready, t + 1)
                    sp.dma_start(table[bass.ds(t * P, P), :], hrow[:, j, :]).then_inc(h_stored[j], 16)
            for j in range(B1):
                sp.wait_ge(h_stored[j], 16 * (NB // B1))
            sp.wait_ge(edges_padded, 64)

        @block.gpsimd
        def _(pool):
            own = Steps(pool, pool_made)
            own.do(nc.gpsimd.memset(ident[:], 0.0))
            own.do(nc.gpsimd.memset(upper_f[:], 0.0))
            own.do(nc.gpsimd.memset(next_row[:], 0.0))
            own.do(nc.gpsimd.memset(wrap_row[:], 0.0))
            own.settle()
            own.do(nc.gpsimd.affine_select(out=ident[:], in_=ident[:], compare_op=ALU.not_equal, fill=1.0, base=0,
                                           pattern=[[-1, P]], channel_multiplier=1))
            own.do(nc.gpsimd.affine_select(out=upper_f[:], in_=upper_f[:], compare_op=ALU.is_ge, fill=1.0, base=0,
                                           pattern=[[-1, P]], channel_multiplier=1))
            own.do(nc.gpsimd.affine_select(out=next_row[:], in_=next_row[:], compare_op=ALU.not_equal, fill=1.0,
                                           base=-1, pattern=[[-1, P]], channel_multiplier=1))
            own.do(nc.gpsimd.affine_select(out=wrap_row[:], in_=wrap_row[:], compare_op=ALU.not_equal, fill=1.0,
                                           base=P - 1, pattern=[[-1, P]], channel_multiplier=P))
            own.do(nc.gpsimd.iota(iota_key[:], [[1, KEYS]], base=0, channel_multiplier=0, allow_small_or_imprecise_dtypes=True))
            own.do(nc.gpsimd.iota(iota_blk[:], [[P, NB]], base=0, channel_multiplier=0, allow_small_or_imprecise_dtypes=True))
            own.do(nc.gpsimd.iota(iota_x[:], [[1, X]], base=0, channel_multiplier=0, allow_small_or_imprecise_dtypes=True))
            own.do(nc.gpsimd.iota(iota_w[:], [[1, W]], base=0, channel_multiplier=0, allow_small_or_imprecise_dtypes=True))
            own.do(nc.gpsimd.iota(node[:], [[P, NB]], base=0, channel_multiplier=1, allow_small_or_imprecise_dtypes=True))
            own.settle()
            own.do(nc.gpsimd.tensor_copy(upper[:], upper_f[:]))
            own.do(nc.gpsimd.memset(ones_b[:], 1.0))
            own.do(nc.gpsimd.memset(ones_f[:], 1.0))
            own.do(nc.gpsimd.memset(eps[:], EPS))
            own.do(nc.gpsimd.memset(row_one[:], 1.0))
            assert own.n == POOL_MADE
            pool.wait_ge(edges_padded, 64)
            pool.wait_ge(seg_found, 1)
            for t in range(NB):
                if t >= SRING:
                    pool.wait_ge(seg_counted, t - SRING + 1)
                nc.gpsimd.indirect_dma_start(seg_row[:, t % SRING, :], None, dst_pad[:, :],
                                             bass.IndirectOffsetOnAxis(ap=seg_at[:, t:t + 1], axis=0)
                                             ).then_inc(seg_gathered[t % SRING], 16)
            pool.wait_ge(adst_ready, NB)
            for k in range(NB // B1):
                pool.wait_ge(position_ready, k + 1)
                for j in range(B1):
                    t = k * B1 + j
                    nc.gpsimd.indirect_dma_start(records[:, :], bass.IndirectOffsetOnAxis(ap=position_i[:, t:t + 1], axis=0),
                                                 rec[:, t, :], None).then_inc(records_stored, 16)
            pool.wait_ge(records_stored, 16 * NB)

        @block.vector
        def _(dve):
            own = Steps(dve, vec)
            nc.vector.memset(zrow[0:1, :], 0).then_inc(pads_ready, 1)
            nc.vector.memset(zrow[32:33, :], 1 << 20).then_inc(pads_ready, 1)
            nc.vector.memset(rec[:, NB - 1, :], 0.0).then_inc(pads_ready, 1)
            own.do(nc.vector.memset(rec[:, 0:NB - 1, C_ID + 1], 0.0))
            own.do(nc.vector.memset(start[:, NB:NB + 1], float(E)))
            own.do(nc.vector.memset(carry[:], 1.0))
            own.settle()
            own.do(nc.vector.memset(carry[:, :, 0:1], 0.0))
            dve.wait_ge(tail_loaded, 16)
            nc.vector.tensor_copy(tail_f[:], tail_i[:]).then_inc(tail_row_ready, 1)
            dve.wait_ge(tail_spread, 1)
            dve.wait_ge(pool_made, POOL_MADE)
            def count_tails(k):
                for j in range(B1):
                    c = bass.ds(k * B1 + j, 1)
                    after(dve, vec_b, k * B1 + max(j - 1, 0))
                    nc.vector.tensor_scalar(junk[:, j % 2, 0:NSEG], ps_tail[:, 0:NSEG], node[:, c], 0.0, ALU.is_lt, ALU.add,
                                            accum_out=full_seg[:, c]).then_inc(vec_b, 1)

            peeled(nc.vector, NB // B1, count_tails)
            dve.wait_ge(vec_b, NB)
            nc.vector.tensor_scalar(seg_at[:], full_seg[:], float(SEG), None, ALU.mult).then_inc(seg_found, 1)
            dve.wait_ge(w_loaded, 16 * (DC + 2))
            for c in range(DC):
                for i in range(2):
                    dve.wait_ge(w_ready, 2 * c)
                    own.do(nc.vector.tensor_tensor(watt[:, i, :], w_sb[:, c, 0:D], att[:, i, :], ALU.mult))
                own.settle()
                for i in range(2):
                    nc.vector.tensor_reduce(w_sb[:, c, D + i * H:D + (i + 1) * H],
                                            watt[:, i, :].rearrange("p (h d) -> p h d", h=H), AX.X, ALU.add
                                            ).then_inc(w_ready, 1)
            dve.wait_ge(x_loaded, 16 * (NB // B1 + 1))
            with nc.vector.Fori(0, NB // B1) as k:
                for j in range(B1):
                    t = bass.ds(k * B1 + j, 1)
                    nc.vector.bn_stats(stats[:, t, :].rearrange("p o s -> p (o s)"),
                                       rec[:, t, 0:D].rearrange("p o d -> p (o d)")).then_inc(tile_stats, 1)
            dve.wait_ge(tile_stats, NB)
            own.do(nc.vector.tensor_tensor(mean[:], stats[:, :, 1], stats[:, :, 4], ALU.add))
            own.do(nc.vector.tensor_tensor(gap[:], stats[:, :, 1], stats[:, :, 4], ALU.subtract))
            own.do(nc.vector.tensor_tensor(spread[:], stats[:, :, 2], stats[:, :, 5], ALU.add))
            own.settle()
            own.do(nc.vector.tensor_tensor(gap[:], gap[:], gap[:], ALU.mult))
            own.do(nc.vector.tensor_scalar(mean[:], mean[:], 0.5, None, ALU.mult))
            own.settle()
            nc.vector.scalar_tensor_tensor(out=spread[:], in0=gap[:], scalar=D / 4.0, in1=spread[:],
                                           op0=ALU.mult, op1=ALU.add).then_inc(var_ready, 1)
            dve.wait_ge(std_ready, 1)
            own.do(nc.vector.reciprocal(rstd[:], std[:]))
            own.settle()

            def normalise(k):
                for j in range(B1):
                    t = bass.ds(k * B1 + j, 1)
                    after(dve, xn_turned, (k - 1) * B1 + j + 1)
                    nc.vector.tensor_scalar(xn[:, j, :], rec[:, t, 0:D].rearrange("p o d -> p (o d)"),
                                            mean[:, t], rstd[:, t], ALU.subtract, ALU.mult).then_inc(xn_ready, 1)
                    dve.wait_ge(seg_gathered[j], 16 * (k + 1))
                    after(dve, seg_counted, k * B1 + max(j - 1, 0))
                    nc.vector.tensor_scalar(junk[:, j % 2, :], seg_row[:, j, :], node[:, t], 0.0, ALU.is_lt, ALU.add,
                                            accum_out=in_seg[:, t]).then_inc(seg_counted, 1)

            peeled(nc.vector, NB // B1, normalise)
            dve.wait_ge(seg_counted, NB)
            nc.vector.scalar_tensor_tensor(out=start[:, 0:NB], in0=full_seg[:], scalar=float(SEG), in1=in_seg[:],
                                           op0=ALU.mult, op1=ALU.add).then_inc(start_ready, 1)
            dve.wait_ge(start_ready, 1)
            dve.wait_ge(end_spread, 1)
            own.do(nc.vector.tensor_tensor(deg[:], ps_small[:, 0:NB], start[:, 0:NB], ALU.subtract))
            own.settle()
            own.do(nc.vector.tensor_scalar(key[:], deg[:], float(KEYS - 1), -1.0, ALU.min, ALU.mult))
            nc.vector.tensor_reduce(deg_max[:], deg[:], AX.X, ALU.max).then_inc(max_ready, 1)
            own.settle()
            own.do(nc.vector.tensor_scalar(key[:], key[:], float(KEYS - 1), None, ALU.add))
            own.do(nc.vector.tensor_copy(rec[:, :, C_START:C_START + 1].bitcast(I32), start[:, 0:NB].unsqueeze(2)))
            own.do(nc.vector.tensor_copy(rec[:, :, C_DEG], deg[:]))
            own.do(nc.vector.tensor_copy(rec[:, :, C_ID], node[:]))
            own.settle()
            nc.vector.tensor_tensor(classes[:, :, :], iota_key[:].unsqueeze(2).to_broadcast([P, KEYS, NB]),
                                    key[:].unsqueeze(1).to_broadcast([P, KEYS, NB]), ALU.is_equal).then_inc(classes_ready, 1)
            dve.wait_ge(classes_ready, 1)
            nc.vector.tensor_tensor_scan(running.rearrange("p k t -> p (k t)"), carry.rearrange("p k t -> p (k t)"),
                                         classes.rearrange("p k t -> p (k t)"), 0.0, ALU.mult, ALU.add
                                         ).then_inc(running_ready, 1)
            dve.wait_ge(counted, 1)
            own.do(nc.vector.tensor_copy(count[:], ps_small[:, 64:65]))
            own.settle()
            nc.vector.tensor_copy(count_b[:], count[:].to_broadcast([P, P])).then_inc(count_ready, 1)
            dve.wait_ge(upto_ready, 1)
            own.do(nc.vector.tensor_tensor(upto[:], ps_small[:, 66:67], count[:], ALU.add))
            own.settle()
            nc.vector.tensor_scalar(passed[:], iota_blk[:], upto[:, 0:1], None, ALU.is_ge).then_inc(passed_ready, 1)
            for t in range(NB):
                dve.wait_ge(ranked, t + 1)
                if t >= 2:
                    dve.wait_ge(rank_read, t - 1)
                nc.vector.tensor_tensor_reduce(junk[:, t % 2, 0:KEYS], ps_rank[t % 2][:, 0:KEYS], classes[:, :, t], 1.0, 0.0,
                                               ALU.mult, ALU.add, position[:, t:t + 1]).then_inc(rank_read, 1)
                if t % B1 == B1 - 1:
                    dve.wait_ge(rank_read, t + 1)
                    nc.vector.tensor_copy(position_i[:, t - B1 + 1:t + 1], position[:, t - B1 + 1:t + 1]).then_inc(position_ready, 1)
            dve.wait_ge(max_turned, 1)
            own.do(nc.vector.tensor_reduce(deg_top[:], ps_tail[0:1, 0:P], AX.X, ALU.max))
            dve.wait_ge(blocks_counted, 1)
            own.do(nc.vector.tensor_scalar(k_max[:], ps_small[0:1, 128:128 + NB], -1.0, float(KEYS - 1), ALU.mult, ALU.add))
            own.settle()
            own.do(nc.vector.tensor_scalar(k_hit[:], k_max[:], float(KEYS - 1), deg_top[:, 0:1], ALU.is_ge, ALU.mult))
            own.settle()
            own.do(nc.vector.tensor_tensor(k_max[:], k_max[:], k_hit[:], ALU.max))
            own.settle()
            own.do(nc.vector.tensor_scalar(plan_i[:, 2, :], k_max[:], 1.0, None, ALU.max))
            own.do(nc.vector.tensor_scalar(plan_i[:, 3, :], k_max[:], float(GS - 1), float(GS), ALU.add, ALU.max))
            own.settle()
            own.do(nc.vector.tensor_scalar(plan_i[:, 0, :], plan_i[:, 3, :], GS.bit_length() - 1, None, ALU.arith_shift_right))
            own.settle()
            own.do(nc.vector.tensor_scalar(plan_i[:, 3, :], plan_i[:, 0, :], float(GW - 1), None, ALU.add))
            own.do(nc.vector.tensor_scalar(plan_i[:, 2, 0:2], plan_i[:, 0, 0:2], float(GS), None, ALU.mult))
            own.settle()
            own.do(nc.vector.tensor_scalar(plan_i[:, 1, :], plan_i[:, 3, :], GW.bit_length() - 1, None, ALU.arith_shift_right))
            own.settle()
            own.do(nc.vector.tensor_copy(plan_f[:], plan_i[:, 0:3, :]))
            own.do(nc.vector.tensor_copy(plan[:, 0, :], plan_i[:, 2, :]))
            own.settle()
            for i in range(3):
                for p in range(2):
                    own.do(nc.vector.tensor_tensor_scan(plan_t[:, i, p::2], row_one[:, p::2], plan_f[:, i, p::2], 0.0,
                                                        ALU.mult, ALU.add))
            own.settle()
            own.do(nc.vector.tensor_tensor(plan[:, 1:4, :], plan_t[:], plan_f[:], ALU.subtract))
            own.settle()

        @block.scalar
        def _(act):
            act.wait_ge(pool_made, POOL_MADE)
            act.wait_ge(var_ready, 1)
            nc.scalar.activation(std[:], spread[:], ACT.Sqrt, bias=eps[:, 0:1], scale=1.0 / D).then_inc(std_ready, 1)

            def move_out(k):
                def turned(j):
                    act.wait_ge(xn_turned, k * B1 + j + 1)
                    nc.scalar.copy(xnT[:, j % 2, :, :].rearrange("p c n -> p (c n)"), ps_turn[j % 2][:, 0:D]).then_inc(xnT_ready, 1)

                turned(0)
                for j in range(B1):
                    t = k * B1 + j
                    if j + 1 < B1:
                        turned(j + 1)
                    act.wait_ge(projected, t + 1)
                    after(act, h_stored[j], k * 16)
                    nc.scalar.copy(rec[:, bass.ds(t, 1), C_ADST:C_ADST + H].rearrange("p o h -> p (o h)"),
                                   ps_proj[j % 2][:, TROW:WCOL]).then_inc(adst_ready, 1)
                    nc.scalar.copy(hrow[:, j, :], ps_proj[j % 2][:, 0:TROW]).then_inc(hrow_ready, 1)

            peeled(nc.scalar, NB // B1, move_out)

        @block.tensor
        def _(pe):
            pe.wait_ge(pool_made, POOL_MADE)
            pe.wait_ge(tail_row_ready, 1)
            nc.tensor.matmul(ps_tail[:, 0:NSEG], ones_f[:], tail_f[:], start=True, stop=True).then_inc(tail_spread, 1)
            pe.wait_ge(w_ready, 2 * DC)
            def project(k):
                def turn(j):
                    pe.wait_ge(xn_ready, k * B1 + j + 1)
                    after(pe, xnT_ready, k * B1 + (j - 1 if j else -1))
                    for c in range(DC):
                        last = nc.tensor.transpose(ps_turn[j % 2][:, c * P:(c + 1) * P], xn[:, j, c * P:(c + 1) * P], ident[:])
                    last.then_inc(xn_turned, 1)

                turn(0)
                for j in range(B1):
                    if j + 1 < B1:
                        turn(j + 1)
                    pe.wait_ge(xnT_ready, k * B1 + j + 1)
                    after(pe, hrow_ready, k * B1 + (j - 1 if j else 0))
                    for c in range(DC):
                        last = nc.tensor.matmul(ps_proj[j % 2][:, 0:WCOL], xnT[:, j % 2, c, :], w_sb[:, c, :],
                                                start=(c == 0), stop=(c == DC - 1))
                    last.then_inc(projected, 1)

            peeled(nc.tensor, NB // B1, project)
            pe.wait_ge(start_ready, 1)
            nc.tensor.matmul(ps_small[:, 0:NB], next_row[:], start[:, 0:NB], start=True, stop=False)
            nc.tensor.matmul(ps_small[:, 0:NB], wrap_row[:], start[:, 1:NB + 1], start=False, stop=True).then_inc(end_spread, 1)
            pe.wait_ge(classes_ready, 1)
            for t in range(NB):
                last = nc.tensor.matmul(ps_small[:, 64:65], classes[:, :, t], ones_b[:, 0:1], start=(t == 0), stop=(t == NB - 1))
            last.then_inc(counted, 1)
            pe.wait_ge(count_ready, 1)
            nc.tensor.matmul(ps_small[:, 66:67], upper_f[:], count[:], start=True, stop=True).then_inc(upto_ready, 1)
            pe.wait_ge(running_ready, 1)
            for t in range(NB):
                if t >= 2:
                    pe.wait_ge(rank_read, t - 1)
                o = ps_rank[t % 2][:, 0:KEYS]
                nc.tensor.matmul(o, count_b[:], upper_f[:], start=True, stop=False)
                if t > 0:
                    nc.tensor.matmul(o, ones_b[:], running[:, :, t - 1], start=False, stop=False)
                nc.tensor.matmul(o, upper[:], classes[:, :, t], start=False, stop=True).then_inc(ranked, 1)
            pe.wait_ge(passed_ready, 1)
            nc.tensor.matmul(ps_small[0:1, 128:128 + NB], ones_b[:, 0:1], passed[:], start=True, stop=True).then_inc(blocks_counted, 1)
            pe.wait_ge(max_ready, 1)
            nc.tensor.transpose(ps_tail[0:1, 0:P], deg_max[:], ident[:]).then_inc(max_turned, 1)


def attend(nc, outer, g):
    src_pad, table, records, xy, queue_in = (g[k] for k in ("src_pad", "table", "records", "xy", "queue_in"))
    bias, gate_w, gate_b = (g[k] for k in ("bias", "gate_w", "gate_b"))
    ident, upper, ones_b, iota_x, iota_w, eps, plan, arena, bank = (
        g[k] for k in ("ident", "upper", "ones_b", "iota_x", "iota_w", "eps", "plan", "arena", "bank"))
    pick, share, rank, chosen, ids = (g[k] for k in ("pick", "share", "rank", "chosen", "ids"))
    MOST_GROUPS = (E + GS - 1) // GS
    MOST_WINDOWS = (MOST_GROUPS + GW - 1) // GW
    MOST_BEFORE = E // GS + 2 * NB
    MOST_SLOTS = E + 2 * NB
    POOL_STEPS = 3
    WINDOW_STEPS = 14
    BLOCK_STEPS = 10
    GATE_STEPS = 15

    with ExitStack() as ctx:
        def sb(name, shape, dt=F32):
            return ctx.enter_context(nc.sbuf_tensor(name, shape, dt))

        def sem(name):
            return ctx.enter_context(nc.semaphore(name))

        rows = [arena[:, i * W * TROW:(i + 1) * W * TROW].rearrange("p (s r) -> p s r", r=TROW) for i in range(2)]
        recb = sb("recb", [P, 2, RROW])
        zeros = sb("zeros", [P, D])
        starts = sb("starts", [P, NB], I32)
        win_at = sb("win_at", [P, 2], I32)
        win_was = sb("win_was", [P, 2], I32)
        win_next = sb("win_next", [P, 2], I32)
        shift = sb("shift", [P, 2], I32)
        nbr = sb("nbr", [P, 2, W], I32)
        logit = sb("logit", [P, W, H])
        prob = sb("prob", [P, W, H])
        mask = sb("mask", [P, W])
        left = sb("left", [P, 1])
        top = sb("top", [P, H])
        top_new = sb("top_new", [P, H])
        drop = sb("drop", [P, H])
        fade = sb("fade", [P, H])
        denom = sb("denom", [P, H])
        dsum = sb("dsum", [P, H])
        acc = sb("acc", [P, D])
        bias_b = sb("bias_b", [P, D])
        gate_sb = sb("gate_sb", [P, DC, X])
        gate_bb = sb("gate_bb", [P, X])
        xy_out = sb("xy_out", [P, 2, 2 * D])
        total = sb("total", [P, 1])
        neg_mean = sb("neg_mean", [P, 1])
        square = sb("square", [P, D])
        sq_sum = sb("sq_sum", [P, 1])
        std = sb("std2", [P, 1])
        rstd = sb("rstd2", [P, 1])
        yT = sb("yT", [P, DC, P])
        score = sb("score", [P, X])
        best = sb("best", [P, 8])
        best_i = sb("best_i", [P, 8], U32)
        best_f = sb("best_f", [P, TOP])
        gap = sb("gap2", [P, 1])
        ratio = sb("ratio", [P, 1])
        pick_now = sb("pick_now", [P, TOP, X])
        rank_now = sb("rank_now", [P, TOP])
        both = sb("both", [P, X], BF16)
        junk = sb("junk2", [P, TOP, X])

        consts = sem("consts")
        zeros_made = sem("zeros_made")
        cleared = sem("cleared")
        shift_made = sem("shift_made")
        own_pool = [sem(f"own_pool{p}") for p in range(2)]
        starts_loaded = sem("starts_loaded")
        rec_loaded = [sem(f"rec_loaded{p}") for p in range(2)]
        nbr_loaded = [sem(f"nbr_loaded{p}") for p in range(2)]
        rows_gathered = [sem(f"rows_gathered{p}") for p in range(2)]
        weighted = [sem(f"weighted{p}") for p in range(2)]
        group_summed = [sem(f"group_summed{p}") for p in range(2)]
        summed = [sem(f"summed{p}") for p in range(2)]
        sum_taken = [sem(f"sum_taken{p}") for p in range(2)]
        logits_ready = [sem(f"logits_ready{p}") for p in range(2)]
        probs_ready = [sem(f"probs_ready{p}") for p in range(2)]
        win_steps = [sem(f"win_steps{p}") for p in range(2)]
        blk_steps = sem("blk_steps")
        gate_steps = sem("gate_steps")
        mean_ready = sem("mean_ready")
        squared = sem("squared")
        std_ready = sem("std_ready2")
        y_ready = sem("y_ready")
        y_turned = sem("y_turned")
        yT_ready = sem("yT_ready")
        scored = sem("scored")
        gap_ready = sem("gap_ready")
        ratio_ready = sem("ratio_ready")
        both_ready = sem("both_ready")
        queued = sem("queued")
        xy_stored = [sem(f"xy_stored{p}") for p in range(2)]

        ps_sum = [bank[0], bank[1]]
        ps_y = bank[2]
        ps_gate = bank[3]
        ps_rank = bank[4]

        def entry(eng, q, b, high):
            return eng.value_load(plan[0:1, q, bass.ds(b, 1)], min_val=1, max_val=high)

        def slots_of(eng, b):
            return entry(eng, 0, b, MOST_SLOTS)

        def groups_for(eng, slots):
            return eng.snap((slots + (GS - 1)) >> (GS.bit_length() - 1), min_val=1, max_val=MOST_GROUPS)

        def windows_for(eng, slots):
            return eng.snap((slots + (W - 1)) >> (W.bit_length() - 1), min_val=1, max_val=MOST_WINDOWS)

        def before(eng, q, b, high):
            return 0 if isinstance(b, int) and b < 2 else entry(eng, q, b, high)

        def groups_before_of(eng, b):
            return before(eng, 1, b, MOST_BEFORE)

        def windows_before_of(eng, b):
            return before(eng, 2, b, MOST_BEFORE)

        def slots_before_of(eng, b):
            return before(eng, 3, b, MOST_SLOTS)

        def part_in(eng, total, w, size):
            rest = eng.snap(total - w * size)
            return eng.snap((rest - (rest > size) * (rest - size)) & (2 * size - 1), min_val=1, max_val=size)

        block = ctx.enter_context(nc.Block())

        @block.sync
        def _(sp):
            with nc.allow_non_contiguous_dma(reason="one word of each record"):
                sp.dma_start(starts[:].unsqueeze(2), records[:, C_START:C_START + 1].bitcast(I32).rearrange("(b p) o -> p b o", p=P)
                             ).then_inc(starts_loaded, 16)
            sp.dma_start(bias_b[:], bias.rearrange("(o d) -> o d", o=1).partition_broadcast(P)).then_inc(consts, 16)
            sp.dma_start(gate_bb[:], gate_b.rearrange("(o d) -> o d", o=1).partition_broadcast(P)).then_inc(consts, 16)
            sp.dma_start(gate_sb[:], gate_w.rearrange("(c p) x -> p c x", p=P)).then_inc(consts, 16)

            def load(b, p, k):
                after(sp, y_ready, b - 1)
                sp.dma_start(recb[:, p, :], records[bass.ds(b * P, P), :]).then_inc(rec_loaded[p], 16)
                sp.dma_start(queue_in[bass.ds(b * (CLEAR * P), CLEAR * P), :].rearrange("(p r) d -> p r d", p=P),
                             zeros[:].unsqueeze(1).to_broadcast([P, CLEAR, D])).then_inc(cleared, 16)
                if not (isinstance(b, int) and b < 2):
                    sp.dma_start(xy[bass.ds(b * P - 2 * P, P), :], xy_out[:, p, :]).then_inc(xy_stored[p], 16)

            sp.wait_ge(zeros_made, 1)
            alternating(sp, NB, load)
            sp.wait_ge(cleared, 16 * NB)
            for b in range(NB - 2, NB):
                sp.wait_ge(y_ready, b + 1)
                sp.dma_start(xy[b * P:(b + 1) * P, :], xy_out[:, b % 2, :]).then_inc(xy_stored[b % 2], 16)
            for p in range(2):
                sp.wait_ge(xy_stored[p], 16 * ((NB + 1 - p) // 2))

        @block.gpsimd
        def _(pool):
            def fetch_nbrs(p, steps, b):
                at = win_next[:, p:p + 1] if b is None else starts[:, bass.ds(b, 1)]
                steps.settle()
                steps.do(nc.gpsimd.tensor_tensor(win_at[:, p:p + 1], at, shift[:, 0:1], ALU.add))
                steps.settle()
                steps.do(nc.gpsimd.tensor_tensor(win_was[:, p:p + 1], win_at[:, p:p + 1], shift[:, 0:1], ALU.add))
                nc.gpsimd.indirect_dma_start(nbr[:, p, :], None, src_pad[:, :],
                                             bass.IndirectOffsetOnAxis(ap=win_at[:, p:p + 1], axis=0),
                                             bounds_check=E, oob_is_err=False).then_inc(nbr_loaded[p], 16)

            pool.wait_ge(blk_steps, 2)
            nc.gpsimd.memset(shift[:, 0:1], 0).then_inc(shift_made, 1)
            nc.gpsimd.memset(shift[:, 1:2], W).then_inc(shift_made, 1)
            nc.gpsimd.memset(nbr[:, :, :], 0).then_inc(shift_made, 1)
            pool.wait_ge(shift_made, 3)
            pool.wait_ge(starts_loaded, 16)
            fetch_nbrs(0, Steps(pool, own_pool[0]), 0)

            def gather(b, p, k):
                slots = slots_of(pool, b)
                windows_before, slots_before = windows_before_of(pool, b), slots_before_of(pool, b)
                windows = windows_for(pool, slots)
                with nc.gpsimd.Fori(0, windows) as w:
                    with nc.gpsimd.If(w > 0):
                        pool.wait_ge(rows_gathered[p], (w * W + slots_before) * 16)
                        fetch_nbrs(p, Steps(pool, own_pool[p], (w + windows_before) * POOL_STEPS), None)
                    pool.wait_ge(nbr_loaded[p], (w + windows_before + 1) * 16)
                    pool.wait_ge(summed[p], w + windows_before + 1)
                    nc.gpsimd.tensor_tensor(win_next[:, p:p + 1], win_at[:, p:p + 1], shift[:, 1:2], ALU.add
                                            ).then_inc(own_pool[p], 1)
                    rest = pool.snap(slots - w * W)

                    def slot(s):
                        nc.gpsimd.indirect_dma_start(rows[p][:, s, :], None, table[:, :],
                                                     bass.IndirectOffsetOnAxis(ap=nbr[:, p, s:s + 1], axis=0)
                                                     ).then_inc(rows_gathered[p], 16)

                    slot(0)
                    for s in range(1, W):
                        if s == GS and not (isinstance(b, int) and b == NB - 1):
                            with nc.gpsimd.If(w < 1):
                                q = 1 - p
                                if isinstance(b, int) and b == 0:
                                    fetch_nbrs(q, Steps(pool, own_pool[q]), 1)
                                else:
                                    slots_q = slots_before_of(pool, b + 1)
                                    windows_q = windows_before_of(pool, b + 1)
                                    pool.wait_ge(rows_gathered[q], slots_q * 16)
                                    fetch_nbrs(q, Steps(pool, own_pool[q], windows_q * POOL_STEPS), b + 1)
                        with nc.gpsimd.If(rest > s):
                            slot(s)

            alternating(nc.gpsimd, NB, gather)

        @block.vector
        def _(dve):
            for p in range(2):
                nc.vector.memset(rows[p][:, :, D:TROW], 0.0).then_inc(blk_steps, 1)
            nc.vector.memset(chosen[:], 0.0).then_inc(blk_steps, 1)
            nc.vector.memset(zeros[:], 0.0).then_inc(zeros_made, 1)
            dve.wait_ge(blk_steps, 3)
            for p in range(2):
                nc.vector.sem_inc(sum_taken[p], 1)
            dve.wait_ge(consts, 48)

            def gate_pick(b):
                steps = Steps(dve, gate_steps, b * GATE_STEPS)
                dve.wait_ge(scored, b + 1)
                steps.do(nc.vector.tensor_tensor(score[:], ps_gate[:, 0:X], gate_bb[:], ALU.add))
                steps.settle()
                steps.do(nc.vector.tensor_copy(rank_now[:], score[:, 0:TOP]))
                steps.do(nc.vector.max(best[:], score[:]))
                steps.settle()
                nc.vector.tensor_tensor(gap[:], best[:, 1:2], best[:, 0:1], ALU.subtract).then_inc(gap_ready, 1)
                steps.do(nc.vector.max_index(best_i[:], best[:], score[:]))
                steps.settle()
                steps.do(nc.vector.tensor_copy(best_f[:], best_i[:, 0:TOP]))
                steps.settle()
                for c in range(TOP):
                    steps.do(nc.vector.tensor_scalar(pick_now[:, c, :], iota_x[:], best_f[:, c:c + 1], None, ALU.is_equal))
                steps.settle()
                nc.vector.tensor_tensor(both[:], pick_now[:, 0, :], pick_now[:, 1, :], ALU.add).then_inc(both_ready, 1)
                steps.do(nc.vector.tensor_copy(pick[:, :, bass.ds(b, 1), :].rearrange("p c o x -> p c (o x)"), pick_now[:]))
                dve.wait_ge(ratio_ready, b + 1)
                steps.do(nc.vector.tensor_scalar(gap[:], ratio[:], 1.0, None, ALU.add))
                steps.settle()
                steps.do(nc.vector.reciprocal(share[:, bass.ds(b, 1), 0:1].rearrange("p o x -> p (o x)"), gap[:]))
                steps.settle()
                steps.do(nc.vector.tensor_tensor(share[:, bass.ds(b, 1), 1:2].rearrange("p o x -> p (o x)"), ratio[:],
                                                 share[:, bass.ds(b, 1), 0:1].rearrange("p o x -> p (o x)"), ALU.mult))
                return steps

            def gate_rank(b, steps):
                dve.wait_ge(queued, b + 1)
                for c in range(TOP):
                    steps.do(nc.vector.tensor_tensor_reduce(
                        junk[:, c, :], ps_rank[:, 0:X], pick_now[:, c, :], 1.0, 0.0, ALU.mult, ALU.add, rank_now[:, c:c + 1]))
                steps.do(nc.vector.tensor_tensor(chosen[:], chosen[:], both[:], ALU.add))
                steps.settle()
                steps.do(nc.vector.tensor_copy(rank[:, bass.ds(b, 1), :].rearrange("p o x -> p (o x)"), rank_now[:]))
                steps.settle()
                assert steps.n == GATE_STEPS, steps.n

            def attend_block(b, p, k):
                slots = slots_of(dve, b)
                windows_before, slots_before = windows_before_of(dve, b), slots_before_of(dve, b)
                windows, groups = windows_for(dve, slots), groups_for(dve, slots)
                blk = Steps(dve, blk_steps, b * BLOCK_STEPS + 3)
                gate = None
                dve.wait_ge(rec_loaded[p], 16 * (k + 1))
                blk.do(nc.vector.memset(top[:], NEG))
                blk.do(nc.vector.memset(denom[:], 0.0))
                blk.do(nc.vector.memset(acc[:], 0.0))
                blk.do(nc.vector.tensor_copy(left[:], recb[:, p, C_DEG:C_DEG + 1]))
                with nc.vector.Fori(0, windows) as w:
                    n = part_in(dve, groups, w, GW)
                    seen = dve.snap(w + windows_before)
                    win = Steps(dve, win_steps[p], seen * WINDOW_STEPS)
                    blk.settle()
                    dve.wait_ge(rows_gathered[p], (part_in(dve, slots, w, W) + w * W + slots_before) * 16)
                    win.do(nc.vector.tensor_tensor(logit[:], rows[p][:, :, D:TROW],
                                                   recb[:, p, C_ADST:C_ADST + H].unsqueeze(1).to_broadcast([P, W, H]), ALU.add))
                    win.do(nc.vector.tensor_scalar(mask[:], iota_w[:], left[:, 0:1], MASK, ALU.is_ge, ALU.mult))
                    win.settle()
                    win.do(nc.vector.scalar_tensor_tensor(out=logit[:], in0=logit[:], scalar=SLOPE, in1=logit[:],
                                                          op0=ALU.mult, op1=ALU.max))
                    win.settle()
                    win.do(nc.vector.tensor_tensor(logit[:], logit[:], mask[:].unsqueeze(2).to_broadcast([P, W, H]), ALU.add))
                    win.settle()
                    win.do(nc.vector.tensor_reduce(top_new[:], logit[:].rearrange("p s h -> p h s"), AX.X, ALU.max))
                    win.settle()
                    win.do(nc.vector.tensor_tensor(top_new[:], top_new[:], top[:], ALU.max))
                    win.settle()
                    nc.vector.tensor_tensor(drop[:], top[:], top_new[:], ALU.subtract).then_inc(logits_ready[p], 1)
                    nc.vector.tensor_tensor(logit[:], logit[:], top_new[:].unsqueeze(1).to_broadcast([P, W, H]),
                                            ALU.subtract).then_inc(logits_ready[p], 1)
                    win.do(nc.vector.tensor_scalar(left[:], left[:], float(-W), None, ALU.add))
                    dve.wait_ge(logits_ready[p], (seen + 1) * 2)
                    win.do(nc.vector.tensor_copy(top[:], top_new[:]))
                    dve.wait_ge(probs_ready[p], (seen + 1) * 2)
                    win.do(nc.vector.tensor_reduce(dsum[:], prob[:].rearrange("p s h -> p h s"), AX.X, ALU.add))
                    win.do(nc.vector.tensor_tensor(denom[:], denom[:], fade[:], ALU.mult))
                    win.do(nc.vector.tensor_tensor(acc[:].rearrange("p (h d) -> p h d", h=H), acc[:].rearrange("p (h d) -> p h d", h=H),
                                                   fade[:].unsqueeze(2).to_broadcast([P, H, HD]), ALU.mult))
                    win.settle()
                    win.do(nc.vector.tensor_tensor(denom[:], denom[:], dsum[:], ALU.add))
                    with nc.vector.Fori(0, n) as i:
                        i = i.with_bounds(min_val=0, max_val=GW - 1)
                        slots = rows[p][:, bass.ds(i * GS, GS), 0:D].rearrange("p s (h d) -> p s h d", h=H)
                        nc.vector.tensor_tensor(slots, slots, prob[:, bass.ds(i * GS, GS), :].unsqueeze(3).to_broadcast([P, GS, H, HD]),
                                                ALU.mult).then_inc(weighted[p], 1)
                    if not (isinstance(b, int) and b == 0):
                        with nc.vector.If(w < 1):
                            gate = gate_pick(b - 1)
                    dve.wait_ge(summed[p], seen + 2)
                    win.do(nc.vector.tensor_tensor(acc[:], acc[:], ps_sum[p][:, 0:D], ALU.add))
                    win.settle()
                    win.do(nc.vector.tensor_tensor(acc[:], acc[:], ps_sum[p][:, D:2 * D], ALU.add))
                    win.settle()
                    assert win.n == WINDOW_STEPS, win.n
                    nc.vector.sem_inc(sum_taken[p], 1)
                blk.do(nc.vector.tensor_scalar(denom[:], denom[:], 1e-16, None, ALU.add))
                blk.settle()
                blk.do(nc.vector.reciprocal(denom[:], denom[:]))
                blk.settle()
                a3 = acc[:].rearrange("p (h d) -> p h d", h=H)
                blk.do(nc.vector.tensor_tensor(a3, a3, denom[:].unsqueeze(2).to_broadcast([P, H, HD]), ALU.mult))
                blk.settle()
                blk.do(nc.vector.tensor_tensor(acc[:], acc[:], bias_b[:], ALU.add))
                blk.settle()
                after(dve, xy_stored[p], 16 * k)
                blk.do(nc.vector.scalar_tensor_tensor(out=xy_out[:, p, 0:D], in0=acc[:], scalar=0.0, in1=recb[:, p, 0:D],
                                                      op0=ALU.max, op1=ALU.add, accum_out=total[:]))
                blk.settle()
                nc.vector.tensor_scalar(neg_mean[:], total[:], -1.0 / D, None, ALU.mult).then_inc(mean_ready, 1)
                nc.vector.tensor_copy(ids[:, bass.ds(b, 1)], recb[:, p, C_ID:C_ID + 1]).then_inc(mean_ready, 1)
                if gate is not None:
                    gate_rank(b - 1, gate)
                dve.wait_ge(std_ready, b + 1)
                blk.do(nc.vector.reciprocal(rstd[:], std[:]))
                blk.settle()
                nc.vector.tensor_scalar(xy_out[:, p, D:2 * D], xy_out[:, p, 0:D], neg_mean[:, 0:1], rstd[:, 0:1],
                                        ALU.add, ALU.mult).then_inc(y_ready, 1)
                dve.wait_ge(y_ready, b + 1)
                assert blk.n == BLOCK_STEPS, blk.n

            alternating(nc.vector, NB, attend_block)
            gate_rank(NB - 1, gate_pick(NB - 1))

        @block.scalar
        def _(act):
            def gate(b):
                act.wait_ge(y_turned, b + 1)
                nc.scalar.copy(yT[:].rearrange("p c n -> p (c n)"), ps_y[:, 0:D]).then_inc(yT_ready, 1)

            def gate_exp(b):
                act.wait_ge(gap_ready, b + 1)
                nc.scalar.activation(ratio[:], gap[:], ACT.Exp).then_inc(ratio_ready, 1)

            def exps(b, p, k):
                if not (isinstance(b, int) and b == 0):
                    gate(b - 1)
                windows, windows_before = windows_for(act, slots_of(act, b)), windows_before_of(act, b)
                with nc.scalar.Fori(0, windows) as w:
                    seen = act.snap(w + windows_before)
                    act.wait_ge(logits_ready[p], (seen + 1) * 2)
                    nc.scalar.activation(fade[:], drop[:], ACT.Exp).then_inc(probs_ready[p], 1)
                    nc.scalar.activation(prob[:], logit[:], ACT.Exp).then_inc(probs_ready[p], 1)
                    if not (isinstance(b, int) and b == 0):
                        with nc.scalar.If(w < 1):
                            gate_exp(b - 1)
                act.wait_ge(mean_ready, (b + 1) * 2)
                nc.scalar.activation(square[:], xy_out[:, p, 0:D], ACT.Square, bias=neg_mean[:, 0:1],
                                     accum_out=sq_sum[:]).then_inc(squared, 1)
                act.wait_ge(squared, b + 1)
                nc.scalar.activation(std[:], sq_sum[:], ACT.Sqrt, bias=eps[:, 0:1], scale=1.0 / D).then_inc(std_ready, 1)

            alternating(nc.scalar, NB, exps)
            gate(NB - 1)
            gate_exp(NB - 1)

        @block.tensor
        def _(pe):
            for p in range(2):
                nc.tensor.sem_inc(summed[p], 1)
            pe.wait_ge(consts, 48)

            def gate(b, p):
                pe.wait_ge(y_ready, b + 1)
                for c in range(DC):
                    last = nc.tensor.transpose(ps_y[:, c * P:(c + 1) * P], xy_out[:, p, D + c * P:D + (c + 1) * P], ident[:])
                last.then_inc(y_turned, 1)
                pe.wait_ge(yT_ready, b + 1)
                for c in range(DC):
                    last = nc.tensor.matmul(ps_gate[:, 0:X], yT[:, c, :], gate_sb[:, c, :], start=(c == 0), stop=(c == DC - 1))
                last.then_inc(scored, 1)

            def places(b):
                pe.wait_ge(both_ready, b + 1)
                nc.tensor.matmul(ps_rank[:, 0:X], upper[:], both[:], start=True, stop=False)
                nc.tensor.matmul(ps_rank[:, 0:X], ones_b[:], chosen[:], start=False, stop=True).then_inc(queued, 1)

            def sums(b, p, k):
                if not (isinstance(b, int) and b == 0):
                    gate(b - 1, 1 - p)
                slots = slots_of(pe, b)
                groups_before, windows_before = groups_before_of(pe, b), windows_before_of(pe, b)
                windows, groups = windows_for(pe, slots), groups_for(pe, slots)
                with nc.tensor.Fori(0, windows) as w:
                    n = part_in(pe, groups, w, GW)
                    g0 = pe.snap(w * GW + groups_before)
                    pe.wait_ge(sum_taken[p], w + windows_before + 1)

                    def group(i, start):
                        pe.wait_ge(weighted[p], g0 + i + 1)
                        for c in range(0, GS, 2):
                            last = nc.tensor.matmul(ps_sum[p][:, :].rearrange("p (s d) -> p s d", s=2), ident[:],
                                                    rows[p][:, bass.ds(i * GS + c, 2), 0:D],
                                                    start=(start and c == 0), stop=True, skip_group_check=True)
                        last.then_inc(group_summed[p], 1)

                    group(0, True)
                    with nc.tensor.If(n > 1):
                        with nc.tensor.Fori(1, n) as i:
                            group(i.with_bounds(min_val=1, max_val=GW - 1), False)
                    pe.wait_ge(group_summed[p], g0 + n)
                    nc.tensor.sem_inc(summed[p], 1)
                if not (isinstance(b, int) and b == 0):
                    places(b - 1)

            alternating(nc.tensor, NB, sums)
            gate(NB - 1, (NB - 1) % 2)
            places(NB - 1)


def experts(nc, outer, g):
    w1, b1, w2, b2, gamma, beta, out = (g[k] for k in ("w1", "b1", "w2", "b2", "gamma", "beta", "out"))
    xy, queue_in, queue_out = (g[k] for k in ("xy", "queue_in", "queue_out"))
    ident, ones_b, eps, arena, bank = (g[k] for k in ("ident", "ones_b", "eps", "arena", "bank"))
    pick, share, rank, chosen, ids = (g[k] for k in ("pick", "share", "rank", "chosen", "ids"))
    YRING = 4
    STAGES = 2
    RING = 4
    JOIN_STEPS = 2

    with ExitStack() as ctx:
        def sb(name, shape, dt=F32):
            return ctx.enter_context(nc.sbuf_tensor(name, shape, dt))

        def sem(name):
            return ctx.enter_context(nc.semaphore(name))

        w1_sb = arena[:, 0:X * DC * F].rearrange("p (x c f) -> p x c f", x=X, c=DC)
        w2_sb = arena[:, X * DC * F:X * (DC * F + FC * D)].rearrange("p (x c d) -> p x c d", x=X, c=FC)
        b1_cols = sb("b1_cols", [P, X * FC])
        b1_rows = sb("b1_rows", [X * FC, P])
        b2_b = sb("b2_b", [P, X, D])
        gamma_b = sb("gamma_b", [P, D])
        beta_b = sb("beta_b", [P, D])
        iota_fb = sb("iota_fb", [1, FB])
        row_x = sb("row_x", [P, X])
        length = sb("length", [P, X])
        blocks_i = sb("blocks_i", [P, X], I32)
        blocks_f = sb("blocks_f", [P, X])
        ends = sb("ends", [P, X])
        base = sb("base", [P, X])
        picked = sb("picked", [P, NB, X])
        owner_f = sb("owner_f", [1, FB])
        owner = sb("owner", [1, FB], I32)
        slot_f = sb("slot_f", [P, TOP, NB])
        slot = sb("slot", [P, TOP, NB], I32)
        y_ring = sb("y_ring", [P, YRING, D])
        rows_in = sb("rows_in", [P, 2, D])
        xT = sb("xT", [P, 2, DC, P])
        hT = sb("hT", [P, 2, FC, P])
        rows_out = sb("rows_out", [P, 2, D])
        taken = sb("taken", [P, RING, TOP, D])
        xy_in = sb("xy_in", [P, RING, 2 * D])
        w1_now = xy_in[:, :, :].rearrange("p r d -> p (r d)").rearrange("p (q c f) -> p q c f", q=2, c=DC)
        joined = sb("joined", [P, RING, D])
        final = arena[:, X * (DC * F + FC * D):][:, 0:RING * D].rearrange("p (r d) -> p r d", r=RING)
        through = taken[0:1, :, :, :].rearrange("o r c d -> o (r c d)")[:, 0:FB * X].rearrange("o (j x) -> o j x", x=X)
        square = sb("square3", [P, D])
        total = sb("total3", [P, RING])
        neg_mean = sb("neg_mean3", [P, RING])
        sq_sum = sb("sq_sum3", [P, RING])
        std = sb("std3", [P, RING])
        rstd = sb("rstd3", [P, RING])

        small_loaded = sem("small_loaded")
        weights_loaded = sem("weights_loaded")
        iota_made = sem("iota_made")
        lengths_ready = sem("lengths_ready")
        b1_turned = sem("b1_turned")
        b1_ready = sem("b1_ready")
        plan_steps = sem("plan_steps")
        slots_ready = sem("slots_ready")
        owners_ready = sem("owners_ready")
        y_loaded = [sem(f"y_loaded{i}") for i in range(YRING)]
        dispatched = [sem(f"dispatched{i}") for i in range(YRING)]
        in_loaded = [sem(f"in_loaded{p}") for p in range(2)]
        x_turned = sem("x_turned")
        xT_ready = sem("xT_ready")
        w1_ready = sem("w1_ready")
        up_done = sem("up_done")
        hT_ready = sem("hT_ready")
        down_done = sem("down_done")
        out_ready = sem("out_ready")
        out_stored = [sem(f"out_stored{p}") for p in range(2)]
        taken_loaded = [sem(f"taken_loaded{i}") for i in range(RING)]
        xy_loaded = [sem(f"xy_loaded{i}") for i in range(RING)]
        join_read = sem("join_read")
        join_steps = sem("join_steps")
        end_steps = sem("end_steps")
        mean_ready = sem("mean_ready3")
        squared = sem("squared3")
        std_ready = sem("std_ready3")
        final_ready = sem("final_ready")
        final_stored = [sem(f"final_stored{i}") for i in range(RING)]

        ps_x = [bank[0], bank[1]]
        ps_up = [bank[2], bank[3]]
        ps_down = [bank[4], bank[5]]

        def stepping(eng, n, step):
            first = STAGES + 2
            inside = lambda j: isinstance(j, int) and 0 <= j < n
            for s in range(first):
                step(s, s % 2, inside)
            pairs = (n - first) // 2
            with eng.Fori(0, pairs) as k:
                for i in range(2):
                    step(first + i + 2 * k, (first + i) % 2, lambda j: True)
            for s in range(first + 2 * pairs, n + STAGES):
                step(s, s % 2, inside)

        def expert_of(eng, j):
            return eng.value_load(owner[0:1, bass.ds(j, 1)], min_val=0, max_val=X - 1)

        block = ctx.enter_context(nc.Block())

        @block.sync
        def _(sp):
            sp.dma_start(b1_rows[:], b1.rearrange("x (c p) -> (x c) p", p=P)).then_inc(small_loaded, 16)
            sp.dma_start(b2_b[:].rearrange("p x d -> p (x d)"),
                         b2.rearrange("(o x) d -> o (x d)", o=1).partition_broadcast(P)).then_inc(small_loaded, 16)
            sp.dma_start(gamma_b[:], gamma.rearrange("(o d) -> o d", o=1).partition_broadcast(P)).then_inc(small_loaded, 16)
            sp.dma_start(beta_b[:], beta.rearrange("(o d) -> o d", o=1).partition_broadcast(P)).then_inc(small_loaded, 16)
            for b in range(NB):
                if b >= YRING:
                    sp.wait_ge(dispatched[b % YRING], 16 * TOP * (b // YRING))
                sp.dma_start(y_ring[:, b % YRING, :], xy[b * P:(b + 1) * P, D:2 * D]).then_inc(y_loaded[b % YRING], 16)
            for i in range(YRING):
                sp.wait_ge(dispatched[i], 16 * TOP * ((NB + YRING - 1 - i) // YRING))

            def load(j, p, k):
                after(sp, x_turned, j - 1)
                sp.dma_start(rows_in[:, p, :], queue_in[bass.ds(j * P, P), :]).then_inc(in_loaded[p], 16)

            alternating(nc.sync, FB, load)

            sp.wait_ge(up_done, FB)
            def load_xy(b, p, k):
                after(sp, final_ready, b - RING + 1)
                sp.dma_start(xy_in[:, p, :], xy[bass.ds(b * P, P), :]).then_inc(xy_loaded[p], 16)

            cycling(nc.sync, NB, RING, load_xy)

        @block.gpsimd
        def _(pool):
            nc.gpsimd.iota(iota_fb[:], [[1, FB]], base=0, channel_multiplier=0, allow_small_or_imprecise_dtypes=True
                           ).then_inc(iota_made, 1)
            pool.wait_ge(slots_ready, 1)
            for b in range(NB):
                pool.wait_ge(y_loaded[b % YRING], 16 * (b // YRING + 1))
                for c in range(TOP):
                    nc.gpsimd.indirect_dma_start(queue_in[:, :], bass.IndirectOffsetOnAxis(ap=slot[:, c, b:b + 1], axis=0),
                                                 y_ring[:, b % YRING, :], None).then_inc(dispatched[b % YRING], 16)

            def store(j, p, k):
                pool.wait_ge(out_ready, j + 1)
                nc.gpsimd.dma_start(queue_out[bass.ds(j * P, P), :], rows_out[:, p, :]).then_inc(out_stored[p], 16)

            alternating(nc.gpsimd, FB, store)
            for p in range(2):
                pool.wait_ge(out_stored[p], 16 * ((FB + 1 - p) // 2))

            def finish(b):
                pool.wait_ge(final_ready, b + 1)
                nc.gpsimd.indirect_dma_start(out[:, :], bass.IndirectOffsetOnAxis(ap=ids[:, b:b + 1], axis=0),
                                             final[:, b % RING, :], None, bounds_check=N - 1, oob_is_err=False
                                             ).then_inc(final_stored[b % RING], 16)

            AHEAD = RING - 1
            for b in range(NB):
                if b >= RING:
                    pool.wait_ge(join_read, b - RING + 1)
                for c in range(TOP):
                    nc.gpsimd.indirect_dma_start(taken[:, b % RING, c, :], None, queue_out[:, :],
                                                 bass.IndirectOffsetOnAxis(ap=slot[:, c, b:b + 1], axis=0)
                                                 ).then_inc(taken_loaded[b % RING], 16)
                if b >= AHEAD:
                    finish(b - AHEAD)
            for b in range(NB - AHEAD, NB):
                finish(b)
            for i in range(RING):
                pool.wait_ge(final_stored[i], 16 * ((NB + RING - 1 - i) // RING))

        @block.vector
        def _(dve):
            steps = Steps(dve, plan_steps)
            steps.do(nc.vector.memset(row_x[:], 1.0))
            dve.wait_ge(b1_turned, 1)
            nc.vector.tensor_copy(b1_cols[:], ps_x[0][:, 0:X * FC]).then_inc(b1_ready, 1)
            dve.wait_ge(lengths_ready, 1)
            steps.do(nc.vector.tensor_copy(length[:], ps_up[0][:, 0:X]))
            steps.settle()
            steps.do(nc.vector.tensor_scalar(blocks_i[:], length[:], float(P - 1), None, ALU.add))
            steps.settle()
            steps.do(nc.vector.tensor_scalar(blocks_i[:], blocks_i[:], P.bit_length() - 1, None, ALU.arith_shift_right))
            steps.settle()
            steps.do(nc.vector.tensor_copy(blocks_f[:], blocks_i[:]))
            steps.settle()
            steps.do(nc.vector.tensor_tensor_scan(ends[:], row_x[:], blocks_f[:], 0.0, ALU.mult, ALU.add))
            steps.settle()
            steps.do(nc.vector.tensor_tensor(base[:], ends[:], blocks_f[:], ALU.subtract))
            steps.settle()
            steps.do(nc.vector.tensor_scalar(base[:], base[:], float(P), None, ALU.mult))
            for c in range(TOP):
                steps.settle()
                steps.do(nc.vector.tensor_tensor(picked[:], pick[:, c, :, :], base[:].unsqueeze(1).to_broadcast([P, NB, X]), ALU.mult))
                steps.settle()
                steps.do(nc.vector.tensor_reduce(slot_f[:, c, :], picked[:], AX.X, ALU.add))
                steps.settle()
                steps.do(nc.vector.tensor_tensor(slot_f[:, c, :], slot_f[:, c, :], rank[:, :, c], ALU.add))
            steps.settle()
            nc.vector.tensor_copy(slot[:], slot_f[:]).then_inc(slots_ready, 1)
            dve.wait_ge(iota_made, 1)
            steps.do(nc.vector.tensor_tensor(through[:], iota_fb[:].unsqueeze(2).to_broadcast([1, FB, X]),
                                             ends[0:1, :].unsqueeze(1).to_broadcast([1, FB, X]), ALU.is_ge))
            steps.settle()
            steps.do(nc.vector.tensor_reduce(owner_f[:], through[:], AX.X, ALU.add))
            steps.settle()
            nc.vector.tensor_scalar(owner[:], owner_f[:], float(X - 1), None, ALU.min).then_inc(owners_ready, 1)
            dve.wait_ge(owners_ready, 1)
            dve.wait_ge(small_loaded, 64)

            dve.wait_ge(weights_loaded, 16 * 2 * X)

            def step(s, p, at_hand):
                j = s
                if at_hand(j):
                    e = expert_of(dve, j)
                    after(dve, up_done, j - 1)
                    nc.vector.tensor_copy(w1_now[:, p, :, :], w1_sb[:, bass.ds(e, 1), :, :].rearrange("p o c f -> p (o c) f")
                                          ).then_inc(w1_ready, 1)
                j = s - STAGES
                if at_hand(j):
                    q = p
                    e = expert_of(dve, j)
                    dve.wait_ge(down_done, j + 1)
                    if not (isinstance(j, int) and j < 2):
                        dve.wait_ge(out_stored[q], (j >> 1) * 16)
                    nc.vector.tensor_tensor(rows_out[:, q, :], ps_down[q][:, 0:D],
                                            b2_b[:, bass.ds(e, 1), :].rearrange("p o d -> p (o d)"), ALU.add).then_inc(out_ready, 1)

            stepping(nc.vector, FB, step)

            def join(b, p, k):
                one = Steps(dve, join_steps, b * JOIN_STEPS)
                dve.wait_ge(taken_loaded[p], (k + 1) * 16 * TOP)
                dve.wait_ge(xy_loaded[p], (k + 1) * 16)
                one.do(nc.vector.scalar_tensor_tensor(out=joined[:, p, :], in0=taken[:, p, 0, :],
                                                      scalar=share[:, bass.ds(b, 1), 0:1].rearrange("p o c -> p (o c)"),
                                                      in1=xy_in[:, p, D:2 * D], op0=ALU.mult, op1=ALU.add))
                one.settle()
                one.do(nc.vector.scalar_tensor_tensor(out=joined[:, p, :], in0=taken[:, p, 1, :],
                                                      scalar=share[:, bass.ds(b, 1), 1:2].rearrange("p o c -> p (o c)"),
                                                      in1=joined[:, p, :], op0=ALU.mult, op1=ALU.add, accum_out=total[:, p:p + 1]))
                one.settle()
                nc.vector.sem_inc(join_read, 1)
                nc.vector.tensor_scalar(neg_mean[:, p:p + 1], total[:, p:p + 1], -1.0 / D, None, ALU.mult).then_inc(mean_ready, 1)

            def norm(b, p, k):
                two = Steps(dve, end_steps, b * 4)
                dve.wait_ge(std_ready, b + 1)
                two.do(nc.vector.reciprocal(rstd[:, p:p + 1], std[:, p:p + 1]))
                two.settle()
                two.do(nc.vector.tensor_scalar(joined[:, p, :], joined[:, p, :], neg_mean[:, p:p + 1], rstd[:, p:p + 1],
                                               ALU.add, ALU.mult))
                two.settle()
                two.do(nc.vector.tensor_tensor(joined[:, p, :], joined[:, p, :], gamma_b[:], ALU.mult))
                two.settle()
                two.do(nc.vector.tensor_tensor(joined[:, p, :], joined[:, p, :], beta_b[:], ALU.add))
                two.settle()
                after(dve, final_stored[p], k * 16)
                nc.vector.tensor_tensor(final[:, p, :], joined[:, p, :], xy_in[:, p, 0:D], ALU.add).then_inc(final_ready, 1)

            join(0, 0, 0)

            def both(b, p, k):
                if not (isinstance(b, int) and b == NB - 1):
                    join(b + 1, (p + 1) % RING, k + (p + 1) // RING)
                norm(b, p, k)

            cycling(nc.vector, NB, RING, both)

        @block.scalar
        def _(act):
            for e in range(X):
                b = e * NB // X
                if e > 0:
                    act.wait_ge(y_loaded[b % YRING], 16 * (b // YRING + 1))
                nc.scalar.dma_start(w1_sb[:, e, :, :], w1[e, :, :].rearrange("(c p) f -> p c f", p=P)).then_inc(weights_loaded, 16)
                nc.scalar.dma_start(w2_sb[:, e, :, :], w2[e, :, :].rearrange("(c p) d -> p c d", p=P)).then_inc(weights_loaded, 16)
            act.wait_ge(b1_ready, 1)

            def step(s, p, at_hand):
                j = s
                if at_hand(j):
                    act.wait_ge(x_turned, j + 1)
                    after(act, up_done, j - 1)
                    nc.scalar.copy(xT[:, p, :, :].rearrange("p c n -> p (c n)"), ps_x[p][:, 0:D]).then_inc(xT_ready, 1)
                j = s - 1
                if at_hand(j):
                    e = expert_of(act, j)
                    act.wait_ge(up_done, j + 1)
                    after(act, down_done, j - 1)
                    for c in range(FC):
                        last = nc.scalar.activation(hT[:, 1 - p, c, :], ps_up[1 - p][:, c * P:(c + 1) * P], ACT.Relu,
                                                    bias=b1_cols[:, bass.ds(e * FC + c, 1)])
                    last.then_inc(hT_ready, 1)

            act.wait_ge(owners_ready, 1)
            stepping(nc.scalar, FB, step)

            def spread(b, p, k):
                act.wait_ge(mean_ready, b + 1)
                nc.scalar.activation(square[:], joined[:, p, :], ACT.Square, bias=neg_mean[:, p:p + 1],
                                     accum_out=sq_sum[:, p:p + 1]).then_inc(squared, 1)
                act.wait_ge(squared, b + 1)
                nc.scalar.activation(std[:, p:p + 1], sq_sum[:, p:p + 1], ACT.Sqrt, bias=eps[:, 0:1], scale=1.0 / D
                                     ).then_inc(std_ready, 1)

            cycling(nc.scalar, NB, RING, spread)

        @block.tensor
        def _(pe):
            pe.wait_ge(small_loaded, 64)
            nc.tensor.transpose(ps_x[0][:, 0:X * FC], b1_rows[:], ident[0:X * FC, 0:X * FC]).then_inc(b1_turned, 1)
            nc.tensor.matmul(ps_up[0][:, 0:X], ones_b[:], chosen[:], start=True, stop=True).then_inc(lengths_ready, 1)
            pe.wait_ge(b1_ready, 1)
            pe.wait_ge(owners_ready, 1)
            pe.wait_ge(weights_loaded, 16 * 2 * X)

            def step(s, p, at_hand):
                j = s
                if at_hand(j):
                    k = s // 2 if isinstance(s, int) else s >> 1
                    pe.wait_ge(in_loaded[p], (k + 1) * 16)
                    after(pe, xT_ready, j - 1)
                    for c in range(DC):
                        last = nc.tensor.transpose(ps_x[p][:, c * P:(c + 1) * P], rows_in[:, p, c * P:(c + 1) * P], ident[:])
                    last.then_inc(x_turned, 1)
                j = s - 1
                if at_hand(j):
                    pe.wait_ge(xT_ready, j + 1)
                    pe.wait_ge(w1_ready, j + 1)
                    after(pe, hT_ready, j - 1)
                    for f in range(FC):
                        for c in range(DC):
                            last = nc.tensor.matmul(ps_up[1 - p][:, f * P:(f + 1) * P],
                                                    w1_now[:, 1 - p, c, f * P:(f + 1) * P],
                                                    xT[:, 1 - p, c, :], start=(c == 0), stop=(c == DC - 1))
                    last.then_inc(up_done, 1)
                j = s - STAGES
                if at_hand(j):
                    e = expert_of(pe, j)
                    pe.wait_ge(hT_ready, j + 1)
                    after(pe, out_ready, j - 1)
                    for c in range(FC):
                        last = nc.tensor.matmul(ps_down[p][:, 0:D], hT[:, p, c, :],
                                                w2_sb[:, bass.ds(e, 1), c, :].rearrange("p o d -> p (o d)"),
                                                start=(c == 0), stop=(c == FC - 1))
                    last.then_inc(down_done, 1)

            stepping(nc.tensor, FB, step)


_INS = ["x", "src", "dst", "L0_gnn_W", "L0_gnn_att_src", "L0_gnn_att_dst", "L0_gnn_bias", "L0_ffn_gate_w", "L0_ffn_gate_b",
        "L0_ffn_w1", "L0_ffn_b1", "L0_ffn_w2", "L0_ffn_b2", "L0_ffn_gamma", "L0_ffn_beta"]


def kernel(**inputs):
    import numpy as _np
    import concourse.bacc as _bacc
    from concourse import mybir as _mybir
    from concourse.bass_utils import run_bass_kernel_spmd as _run

    nc = _bacc.Bacc("TRN2", target_bir_lowering=False, num_devices=1)
    arrays, args = {}, []
    for name in _INS:
        a = _np.ascontiguousarray(inputs[name])
        arrays[f"in_{name}_dram"] = a
        args.append(nc.dram_tensor(f"in_{name}_dram", a.shape, _mybir.dt.from_np(a.dtype), kind="ExternalInput").ap())
    args.append(nc.dram_tensor("out_0_dram", (N, D), _mybir.dt.float32, kind="ExternalOutput").ap())
    gnn_ffn_kernel(nc, *args)
    r = _run(nc, [arrays], core_ids=[0])
    return r.results[0]["out_0_dram"]
```

```python
from contextlib import ExitStack

import concourse.bass as bass
from concourse import mybir

ALU = mybir.AluOpType
ACT = mybir.ActivationFunctionType
AX = mybir.AxisListType
F32 = mybir.dt.float32
BF16 = mybir.dt.bfloat16
I32 = mybir.dt.int32
U32 = mybir.dt.uint32

P = 128
N = 6250
E = 206250
D = 256
H = 8
HD = D // H
NB = (N + P - 1) // P
NPAD = NB * P
LAST = N - (NB - 1) * P
EPS = 1e-5
SLOPE = 0.2

TROW = D + H
WCOL = D + 2 * H
RROW = D + H + 4
C_ADST, C_START, C_DEG, C_ID = D, D + H, D + H + 1, D + H + 2

SEG = 454
NSEG = E // SEG
KEYS = P

GS = 4
W = 64
GW = W // GS
EDGE_PAD = SEG + W
NEG = -1.0e30
MASK = -2.0e30

X = 16
F = 512
FC = F // P
DC = D // P
TOP = 2
YRING = 4
PART = 29
FB = (TOP * N + 2 * X * (P - 1)) // P
LEAST = (TOP * N + P - 1) // P
CAP = FB + 6
LEAST_0 = TOP * PART
MOST_0 = (TOP * PART * P + X * (P - 1)) // P
CLEAR = (CAP + NB - 1) // NB
CLEAR_OUT = (CAP - LEAST_0 + NB - 1) // NB

B1 = 7
SRING = B1


class Steps:

    def __init__(self, eng, sem, base=0):
        self.eng, self.sem, self.base, self.n = eng, sem, base, 0

    def do(self, ins):
        ins.then_inc(self.sem, 1)
        self.n += 1

    def settle(self):
        after(self.eng, self.sem, self.base + self.n)


def after(eng, sem, value):
    if not isinstance(value, int) or value > 0:
        eng.wait_ge(sem, value)


def peeled(eng, n, body):
    body(0)
    with eng.Fori(1, n) as k:
        body(k)


def alternating(eng, n, body):
    body(0, 0, 0)
    body(1, 1, 0)
    with eng.Fori(1, n // 2) as k:
        body(2 * k, 0, k)
        body(2 * k + 1, 1, k)
    for i in range(n // 2 * 2, n):
        body(i, i % 2, i // 2)


def gnn_ffn_kernel(nc, x, src, dst, w, att_src, att_dst, bias, gate_w, gate_b, w1, b1, w2, b2, gamma, beta, out):
    src_pad = nc.dram_tensor("src_pad", [E + EDGE_PAD, 1], I32).ap()
    dst_pad = nc.dram_tensor("dst_pad", [E + EDGE_PAD, 1], I32).ap()
    table = nc.dram_tensor("table", [NPAD, TROW], F32).ap()
    records = nc.dram_tensor("records", [NPAD, RROW], F32).ap()
    xy = nc.dram_tensor("xy", [NPAD, 2 * D], F32).ap()
    queue_in = nc.dram_tensor("queue_in", [NB * CLEAR * P, D], F32).ap()
    queue_out = nc.dram_tensor("queue_out", [(LEAST_0 + NB * CLEAR_OUT) * P, D], F32).ap()

    with ExitStack() as ctx:
        def sb(name, shape, dt=F32):
            return ctx.enter_context(nc.sbuf_tensor(name, shape, dt))

        def sem(name):
            return ctx.enter_context(nc.semaphore(name))

        bank = [ctx.enter_context(nc.psum_tensor(f"bank{i}", [P, 512], F32)) for i in range(8)]

        ident = sb("ident", [P, P])
        upper = sb("upper", [P, P], BF16)
        ones_b = sb("ones_b", [P, P], BF16)
        iota_x = sb("iota_x", [P, X])
        iota_w = sb("iota_w", [P, W])
        eps = sb("eps", [P, 1])
        plan = sb("plan", [1, 4, NB], I32)
        arena = sb("arena", [P, 2 * W * TROW])
        rec = arena[:, 0:NB * RROW].rearrange("p (b r) -> p b r", r=RROW)

        pick = sb("pick", [P, TOP, NB, X])
        share = sb("share", [P, NB, TOP])
        rank = sb("rank", [P, NB, TOP])
        chosen = sb("chosen", [P, 2, X], BF16)
        ids = sb("ids", [P, NB], I32)
        slot = sb("slot", [P, TOP, NB], I32)

        build_graph(nc, ctx, locals())
        attend(nc, ctx, locals())
        experts(nc, ctx, locals())


def build_graph(nc, outer, g):
    x, src, dst, w, att_src, att_dst = (g[k] for k in ("x", "src", "dst", "w", "att_src", "att_dst"))
    src_pad, dst_pad, table, records = (g[k] for k in ("src_pad", "dst_pad", "table", "records"))
    ident, upper, ones_b, iota_x, iota_w, eps, plan, arena, rec, bank = (
        g[k] for k in ("ident", "upper", "ones_b", "iota_x", "iota_w", "eps", "plan", "arena", "rec", "bank"))
    EDGE_ROWS = 250
    at = [NB * RROW]

    with ExitStack() as ctx:
        def sb(name, shape, dt=F32):
            return ctx.enter_context(nc.sbuf_tensor(name, shape, dt))

        def sem(name):
            return ctx.enter_context(nc.semaphore(name))

        def spare(words):
            a = arena[:, at[0]:at[0] + words]
            at[0] += words
            assert at[0] <= 2 * W * TROW
            return a

        upper_f = sb("upper_f", [P, P])
        iota_key = sb("iota_key", [P, KEYS])
        iota_blk = sb("iota_blk", [P, NB])
        node = sb("node", [P, NB])
        next_row = sb("next_row", [P, P])
        wrap_row = sb("wrap_row", [P, P])
        w_sb = sb("w_sb", [P, DC, WCOL])
        att = sb("att", [P, 2, D])
        watt = sb("watt", [P, 2, D])
        stats = sb("stats", [P, NB, 6])
        mean = sb("mean", [P, NB])
        gap = sb("gap", [P, NB])
        spread = sb("spread", [P, NB])
        std = sb("std", [P, NB])
        rstd = sb("rstd", [P, NB])
        xn = spare(B1 * D).rearrange("p (b d) -> p b d", b=B1)
        xnT = spare(2 * D).rearrange("p (b c n) -> p b c n", b=2, c=DC)
        hrow = spare(B1 * TROW).rearrange("p (b r) -> p b r", b=B1)
        tail_i = sb("tail_i", [1, NSEG], I32)
        tail_f = sb("tail_f", [1, NSEG])
        ones_f = sb("ones_f", [1, P])
        full_seg = sb("full_seg", [P, NB])
        seg_at = sb("seg_at", [P, NB], I32)
        seg_row = spare(SRING * SEG).bitcast(I32).rearrange("p (r s) -> p r s", r=SRING)
        junk = spare(2 * SEG).rearrange("p (b s) -> p b s", b=2)
        in_seg = sb("in_seg", [P, NB])
        start = sb("start", [P, NB + 1])
        deg = sb("deg", [P, NB])
        key = sb("key", [P, NB])
        classes = spare(KEYS * NB // 2).bitcast(BF16).rearrange("p (k t) -> p k t", k=KEYS)
        carry = spare(KEYS * NB // 2).bitcast(BF16).rearrange("p (k t) -> p k t", k=KEYS)
        running = spare(KEYS * NB // 2).bitcast(BF16).rearrange("p (k t) -> p k t", k=KEYS)
        count = sb("count", [P, 1])
        count_b = sb("count_b", [P, P])
        upto = sb("upto", [P, 1])
        passed = sb("passed", [P, NB], BF16)
        position = sb("position", [P, NB])
        position_i = sb("position_i", [P, NB], I32)
        deg_max = sb("deg_max", [P, 1])
        deg_top = sb("deg_top", [1, 1])
        k_max = sb("k_max", [1, NB])
        k_hit = sb("k_hit", [1, NB])
        plan_i = sb("plan_i", [1, 4, NB], I32)
        plan_f = sb("plan_f", [1, 3, NB])
        plan_t = sb("plan_t", [1, 3, NB])
        row_one = sb("row_one", [1, NB])
        zrow = sb("zrow", [P, EDGE_PAD], I32)

        x_loaded = sem("x_loaded")
        w_loaded = sem("w_loaded")
        tail_loaded = sem("tail_loaded")
        edges_padded = sem("edges_padded")
        pads_ready = sem("pads_ready")
        pool_made = sem("pool_made")
        vec = sem("vec")
        vec_b = sem("vec_b")
        tail_row_ready = sem("tail_row_ready")
        tail_spread = sem("tail_spread")
        seg_found = sem("seg_found")
        seg_gathered = [sem(f"seg_gathered{i}") for i in range(SRING)]
        seg_counted = sem("seg_counted")
        w_ready = sem("w_ready")
        tile_stats = sem("tile_stats")
        var_ready = sem("var_ready")
        std_ready = sem("std_ready")
        xn_ready = sem("xn_ready")
        xn_turned = sem("xn_turned")
        xnT_ready = sem("xnT_ready")
        projected = sem("projected")
        hrow_ready = sem("hrow_ready")
        adst_ready = sem("adst_ready")
        h_stored = [sem(f"h_stored{j}") for j in range(B1)]
        start_ready = sem("start_ready")
        end_spread = sem("end_spread")
        classes_ready = sem("classes_ready")
        counted = sem("counted")
        count_ready = sem("count_ready")
        upto_ready = sem("upto_ready")
        passed_ready = sem("passed_ready")
        blocks_counted = sem("blocks_counted")
        max_ready = sem("max_ready")
        max_turned = sem("max_turned")
        running_ready = sem("running_ready")
        ranked = sem("ranked")
        rank_read = sem("rank_read")
        position_ready = sem("position_ready")
        records_stored = sem("records_stored")

        ps_turn = [bank[0], bank[1]]
        ps_proj = [bank[2], bank[3]]
        ps_tail = bank[4]
        ps_small = bank[5]
        ps_rank = [bank[6], bank[7]]
        POOL_MADE = 18

        block = ctx.enter_context(nc.Block())

        @block.sync
        def _(sp):
            with nc.allow_non_contiguous_dma(reason="one dst of each segment"):
                tails = dst[0:NSEG * SEG].rearrange("(o j s) -> o j s", o=1, s=SEG)[:, :, SEG - 1:SEG]
                sp.dma_start(tail_i[0:1, :].rearrange("o (j s) -> o j s", s=1), tails).then_inc(tail_loaded, 16)
            for a, b in ((src, src_pad), (dst, dst_pad)):
                sp.dma_start(b[0:E, :].rearrange("(r c) o -> r (c o)", r=EDGE_ROWS),
                             a.rearrange("(r c) -> r c", r=EDGE_ROWS)).then_inc(edges_padded, 16)
            sp.wait_ge(pads_ready, 2)
            sp.dma_start(src_pad[E:E + EDGE_PAD, :].rearrange("(o c) e -> o (c e)", o=1),
                         zrow[0:1, :]).then_inc(edges_padded, 16)
            sp.dma_start(dst_pad[E:E + EDGE_PAD, :].rearrange("(o c) e -> o (c e)", o=1),
                         zrow[32:33, :]).then_inc(edges_padded, 16)
            for c in range(DC):
                sp.dma_start(w_sb[:, c, 0:D], w.rearrange("f h d -> f (h d)")[c * P:(c + 1) * P, :]).then_inc(w_loaded, 16)
            for i, a in enumerate((att_src, att_dst)):
                sp.dma_start(att[:, i, :], a.rearrange("(o h) d -> o (h d)", o=1).partition_broadcast(P)).then_inc(w_loaded, 16)
            sp.wait_ge(pads_ready, 3)
            for k in range(NB // B1):
                n_full = B1 if k < NB // B1 - 1 else B1 - 1
                t0 = k * B1
                sp.dma_start(rec[:, t0:t0 + n_full, 0:D],
                             x[t0 * P:(t0 + n_full) * P, :].rearrange("(t p) d -> p t d", p=P)).then_inc(x_loaded, 16)
            sp.dma_start(rec[0:LAST, NB - 1, 0:D], x[(NB - 1) * P:N, :]).then_inc(x_loaded, 16)
            with nc.sync.Fori(0, NB // B1) as k:
                for j in range(B1):
                    t = k * B1 + j
                    sp.wait_ge(hrow_ready, t + 1)
                    sp.dma_start(table[bass.ds(t * P, P), :], hrow[:, j, :]).then_inc(h_stored[j], 16)
            for j in range(B1):
                sp.wait_ge(h_stored[j], 16 * (NB // B1))
            sp.wait_ge(edges_padded, 64)

        @block.gpsimd
        def _(pool):
            own = Steps(pool, pool_made)
            own.do(nc.gpsimd.memset(ident[:], 0.0))
            own.do(nc.gpsimd.memset(upper_f[:], 0.0))
            own.do(nc.gpsimd.memset(next_row[:], 0.0))
            own.do(nc.gpsimd.memset(wrap_row[:], 0.0))
            own.settle()
            own.do(nc.gpsimd.affine_select(out=ident[:], in_=ident[:], compare_op=ALU.not_equal, fill=1.0, base=0,
                                           pattern=[[-1, P]], channel_multiplier=1))
            own.do(nc.gpsimd.affine_select(out=upper_f[:], in_=upper_f[:], compare_op=ALU.is_ge, fill=1.0, base=0,
                                           pattern=[[-1, P]], channel_multiplier=1))
            own.do(nc.gpsimd.affine_select(out=next_row[:], in_=next_row[:], compare_op=ALU.not_equal, fill=1.0,
                                           base=-1, pattern=[[-1, P]], channel_multiplier=1))
            own.do(nc.gpsimd.affine_select(out=wrap_row[:], in_=wrap_row[:], compare_op=ALU.not_equal, fill=1.0,
                                           base=P - 1, pattern=[[-1, P]], channel_multiplier=P))
            own.do(nc.gpsimd.iota(iota_key[:], [[1, KEYS]], base=0, channel_multiplier=0, allow_small_or_imprecise_dtypes=True))
            own.do(nc.gpsimd.iota(iota_blk[:], [[P, NB]], base=0, channel_multiplier=0, allow_small_or_imprecise_dtypes=True))
            own.do(nc.gpsimd.iota(iota_x[:], [[1, X]], base=0, channel_multiplier=0, allow_small_or_imprecise_dtypes=True))
            own.do(nc.gpsimd.iota(iota_w[:], [[1, W]], base=0, channel_multiplier=0, allow_small_or_imprecise_dtypes=True))
            own.do(nc.gpsimd.iota(node[:], [[P, NB]], base=0, channel_multiplier=1, allow_small_or_imprecise_dtypes=True))
            own.settle()
            own.do(nc.gpsimd.tensor_copy(upper[:], upper_f[:]))
            own.do(nc.gpsimd.memset(ones_b[:], 1.0))
            own.do(nc.gpsimd.memset(ones_f[:], 1.0))
            own.do(nc.gpsimd.memset(eps[:], EPS))
            own.do(nc.gpsimd.memset(row_one[:], 1.0))
            assert own.n == POOL_MADE
            pool.wait_ge(edges_padded, 64)
            pool.wait_ge(seg_found, 1)
            for t in range(NB):
                if t >= SRING:
                    pool.wait_ge(seg_counted, t - SRING + 1)
                nc.gpsimd.indirect_dma_start(seg_row[:, t % SRING, :], None, dst_pad[:, :],
                                             bass.IndirectOffsetOnAxis(ap=seg_at[:, t:t + 1], axis=0)
                                             ).then_inc(seg_gathered[t % SRING], 16)
            pool.wait_ge(adst_ready, NB)
            for k in range(NB // B1):
                pool.wait_ge(position_ready, k + 1)
                for j in range(B1):
                    t = k * B1 + j
                    nc.gpsimd.indirect_dma_start(records[:, :], bass.IndirectOffsetOnAxis(ap=position_i[:, t:t + 1], axis=0),
                                                 rec[:, t, :], None).then_inc(records_stored, 16)
            pool.wait_ge(records_stored, 16 * NB)

        @block.vector
        def _(dve):
            own = Steps(dve, vec)
            nc.vector.memset(zrow[0:1, :], 0).then_inc(pads_ready, 1)
            nc.vector.memset(zrow[32:33, :], 1 << 20).then_inc(pads_ready, 1)
            nc.vector.memset(rec[:, NB - 1, :], 0.0).then_inc(pads_ready, 1)
            own.do(nc.vector.memset(rec[:, 0:NB - 1, C_ID + 1], 0.0))
            own.do(nc.vector.memset(start[:, NB:NB + 1], float(E)))
            own.do(nc.vector.memset(carry[:], 1.0))
            own.settle()
            own.do(nc.vector.memset(carry[:, :, 0:1], 0.0))
            dve.wait_ge(tail_loaded, 16)
            nc.vector.tensor_copy(tail_f[:], tail_i[:]).then_inc(tail_row_ready, 1)
            dve.wait_ge(tail_spread, 1)
            dve.wait_ge(pool_made, POOL_MADE)
            def count_tails(k):
                for j in range(B1):
                    c = bass.ds(k * B1 + j, 1)
                    after(dve, vec_b, k * B1 + max(j - 1, 0))
                    nc.vector.tensor_scalar(junk[:, j % 2, 0:NSEG], ps_tail[:, 0:NSEG], node[:, c], 0.0, ALU.is_lt, ALU.add,
                                            accum_out=full_seg[:, c]).then_inc(vec_b, 1)

            peeled(nc.vector, NB // B1, count_tails)
            dve.wait_ge(vec_b, NB)
            nc.vector.tensor_scalar(seg_at[:], full_seg[:], float(SEG), None, ALU.mult).then_inc(seg_found, 1)
            dve.wait_ge(w_loaded, 16 * (DC + 2))
            for c in range(DC):
                for i in range(2):
                    dve.wait_ge(w_ready, 2 * c)
                    own.do(nc.vector.tensor_tensor(watt[:, i, :], w_sb[:, c, 0:D], att[:, i, :], ALU.mult))
                own.settle()
                for i in range(2):
                    nc.vector.tensor_reduce(w_sb[:, c, D + i * H:D + (i + 1) * H],
                                            watt[:, i, :].rearrange("p (h d) -> p h d", h=H), AX.X, ALU.add
                                            ).then_inc(w_ready, 1)
            dve.wait_ge(x_loaded, 16 * (NB // B1 + 1))
            with nc.vector.Fori(0, NB // B1) as k:
                for j in range(B1):
                    t = bass.ds(k * B1 + j, 1)
                    nc.vector.bn_stats(stats[:, t, :].rearrange("p o s -> p (o s)"),
                                       rec[:, t, 0:D].rearrange("p o d -> p (o d)")).then_inc(tile_stats, 1)
            dve.wait_ge(tile_stats, NB)
            own.do(nc.vector.tensor_tensor(mean[:], stats[:, :, 1], stats[:, :, 4], ALU.add))
            own.do(nc.vector.tensor_tensor(gap[:], stats[:, :, 1], stats[:, :, 4], ALU.subtract))
            own.do(nc.vector.tensor_tensor(spread[:], stats[:, :, 2], stats[:, :, 5], ALU.add))
            own.settle()
            own.do(nc.vector.tensor_tensor(gap[:], gap[:], gap[:], ALU.mult))
            own.do(nc.vector.tensor_scalar(mean[:], mean[:], 0.5, None, ALU.mult))
            own.settle()
            nc.vector.scalar_tensor_tensor(out=spread[:], in0=gap[:], scalar=D / 4.0, in1=spread[:],
                                           op0=ALU.mult, op1=ALU.add).then_inc(var_ready, 1)
            dve.wait_ge(std_ready, 1)
            own.do(nc.vector.reciprocal(rstd[:], std[:]))
            own.settle()

            def normalise(k):
                for j in range(B1):
                    t = bass.ds(k * B1 + j, 1)
                    after(dve, xn_turned, (k - 1) * B1 + j + 1)
                    nc.vector.tensor_scalar(xn[:, j, :], rec[:, t, 0:D].rearrange("p o d -> p (o d)"),
                                            mean[:, t], rstd[:, t], ALU.subtract, ALU.mult).then_inc(xn_ready, 1)
                    dve.wait_ge(seg_gathered[j], 16 * (k + 1))
                    after(dve, seg_counted, k * B1 + max(j - 1, 0))
                    nc.vector.tensor_scalar(junk[:, j % 2, :], seg_row[:, j, :], node[:, t], 0.0, ALU.is_lt, ALU.add,
                                            accum_out=in_seg[:, t]).then_inc(seg_counted, 1)

            peeled(nc.vector, NB // B1, normalise)
            dve.wait_ge(seg_counted, NB)
            nc.vector.scalar_tensor_tensor(out=start[:, 0:NB], in0=full_seg[:], scalar=float(SEG), in1=in_seg[:],
                                           op0=ALU.mult, op1=ALU.add).then_inc(start_ready, 1)
            dve.wait_ge(start_ready, 1)
            dve.wait_ge(end_spread, 1)
            own.do(nc.vector.tensor_tensor(deg[:], ps_small[:, 0:NB], start[:, 0:NB], ALU.subtract))
            own.settle()
            own.do(nc.vector.tensor_scalar(key[:], deg[:], float(KEYS - 1), -1.0, ALU.min, ALU.mult))
            nc.vector.tensor_reduce(deg_max[:], deg[:], AX.X, ALU.max).then_inc(max_ready, 1)
            own.settle()
            own.do(nc.vector.tensor_scalar(key[:], key[:], float(KEYS - 1), None, ALU.add))
            own.do(nc.vector.tensor_copy(rec[:, :, C_START:C_START + 1].bitcast(I32), start[:, 0:NB].unsqueeze(2)))
            own.do(nc.vector.tensor_copy(rec[:, :, C_DEG], deg[:]))
            own.do(nc.vector.tensor_copy(rec[:, :, C_ID], node[:]))
            own.settle()
            nc.vector.tensor_tensor(classes[:, :, :], iota_key[:].unsqueeze(2).to_broadcast([P, KEYS, NB]),
                                    key[:].unsqueeze(1).to_broadcast([P, KEYS, NB]), ALU.is_equal).then_inc(classes_ready, 1)
            dve.wait_ge(classes_ready, 1)
            nc.vector.tensor_tensor_scan(running.rearrange("p k t -> p (k t)"), carry.rearrange("p k t -> p (k t)"),
                                         classes.rearrange("p k t -> p (k t)"), 0.0, ALU.mult, ALU.add
                                         ).then_inc(running_ready, 1)
            dve.wait_ge(counted, 1)
            own.do(nc.vector.tensor_copy(count[:], ps_small[:, 64:65]))
            own.settle()
            nc.vector.tensor_copy(count_b[:], count[:].to_broadcast([P, P])).then_inc(count_ready, 1)
            dve.wait_ge(upto_ready, 1)
            own.do(nc.vector.tensor_tensor(upto[:], ps_small[:, 66:67], count[:], ALU.add))
            own.settle()
            nc.vector.tensor_scalar(passed[:], iota_blk[:], upto[:, 0:1], None, ALU.is_ge).then_inc(passed_ready, 1)
            for t in range(NB):
                dve.wait_ge(ranked, t + 1)
                if t >= 2:
                    dve.wait_ge(rank_read, t - 1)
                nc.vector.tensor_tensor_reduce(junk[:, t % 2, 0:KEYS], ps_rank[t % 2][:, 0:KEYS], classes[:, :, t], 1.0, 0.0,
                                               ALU.mult, ALU.add, position[:, t:t + 1]).then_inc(rank_read, 1)
                if t % B1 == B1 - 1:
                    dve.wait_ge(rank_read, t + 1)
                    nc.vector.tensor_copy(position_i[:, t - B1 + 1:t + 1], position[:, t - B1 + 1:t + 1]).then_inc(position_ready, 1)
            dve.wait_ge(max_turned, 1)
            own.do(nc.vector.tensor_reduce(deg_top[:], ps_tail[0:1, 0:P], AX.X, ALU.max))
            dve.wait_ge(blocks_counted, 1)
            own.do(nc.vector.tensor_scalar(k_max[:], ps_small[0:1, 128:128 + NB], -1.0, float(KEYS - 1), ALU.mult, ALU.add))
            own.settle()
            own.do(nc.vector.tensor_scalar(k_hit[:], k_max[:], float(KEYS - 1), deg_top[:, 0:1], ALU.is_ge, ALU.mult))
            own.settle()
            own.do(nc.vector.tensor_tensor(k_max[:], k_max[:], k_hit[:], ALU.max))
            own.settle()
            own.do(nc.vector.tensor_scalar(plan_i[:, 2, :], k_max[:], 1.0, None, ALU.max))
            own.do(nc.vector.tensor_scalar(plan_i[:, 3, :], k_max[:], float(GS - 1), float(GS), ALU.add, ALU.max))
            own.settle()
            own.do(nc.vector.tensor_scalar(plan_i[:, 0, :], plan_i[:, 3, :], GS.bit_length() - 1, None, ALU.arith_shift_right))
            own.settle()
            own.do(nc.vector.tensor_scalar(plan_i[:, 3, :], plan_i[:, 0, :], float(GW - 1), None, ALU.add))
            own.do(nc.vector.tensor_scalar(plan_i[:, 2, 0:2], plan_i[:, 0, 0:2], float(GS), None, ALU.mult))
            own.settle()
            own.do(nc.vector.tensor_scalar(plan_i[:, 1, :], plan_i[:, 3, :], GW.bit_length() - 1, None, ALU.arith_shift_right))
            own.settle()
            own.do(nc.vector.tensor_copy(plan_f[:], plan_i[:, 0:3, :]))
            own.do(nc.vector.tensor_copy(plan[:, 0, :], plan_i[:, 2, :]))
            own.settle()
            for i in range(3):
                for p in range(2):
                    own.do(nc.vector.tensor_tensor_scan(plan_t[:, i, p::2], row_one[:, p::2], plan_f[:, i, p::2], 0.0,
                                                        ALU.mult, ALU.add))
            own.settle()
            own.do(nc.vector.tensor_tensor(plan[:, 1:4, :], plan_t[:], plan_f[:], ALU.subtract))
            own.settle()

        @block.scalar
        def _(act):
            act.wait_ge(pool_made, POOL_MADE)
            act.wait_ge(var_ready, 1)
            nc.scalar.activation(std[:], spread[:], ACT.Sqrt, bias=eps[:, 0:1], scale=1.0 / D).then_inc(std_ready, 1)

            def move_out(k):
                def turned(j):
                    act.wait_ge(xn_turned, k * B1 + j + 1)
                    nc.scalar.copy(xnT[:, j % 2, :, :].rearrange("p c n -> p (c n)"), ps_turn[j % 2][:, 0:D]).then_inc(xnT_ready, 1)

                turned(0)
                for j in range(B1):
                    t = k * B1 + j
                    if j + 1 < B1:
                        turned(j + 1)
                    act.wait_ge(projected, t + 1)
                    after(act, h_stored[j], k * 16)
                    nc.scalar.copy(rec[:, bass.ds(t, 1), C_ADST:C_ADST + H].rearrange("p o h -> p (o h)"),
                                   ps_proj[j % 2][:, TROW:WCOL]).then_inc(adst_ready, 1)
                    nc.scalar.copy(hrow[:, j, :], ps_proj[j % 2][:, 0:TROW]).then_inc(hrow_ready, 1)

            peeled(nc.scalar, NB // B1, move_out)

        @block.tensor
        def _(pe):
            pe.wait_ge(pool_made, POOL_MADE)
            pe.wait_ge(tail_row_ready, 1)
            nc.tensor.matmul(ps_tail[:, 0:NSEG], ones_f[:], tail_f[:], start=True, stop=True).then_inc(tail_spread, 1)
            pe.wait_ge(w_ready, 2 * DC)
            def project(k):
                def turn(j):
                    pe.wait_ge(xn_ready, k * B1 + j + 1)
                    after(pe, xnT_ready, k * B1 + (j - 1 if j else -1))
                    for c in range(DC):
                        last = nc.tensor.transpose(ps_turn[j % 2][:, c * P:(c + 1) * P], xn[:, j, c * P:(c + 1) * P], ident[:])
                    last.then_inc(xn_turned, 1)

                turn(0)
                for j in range(B1):
                    if j + 1 < B1:
                        turn(j + 1)
                    pe.wait_ge(xnT_ready, k * B1 + j + 1)
                    after(pe, hrow_ready, k * B1 + (j - 1 if j else 0))
                    for c in range(DC):
                        last = nc.tensor.matmul(ps_proj[j % 2][:, 0:WCOL], xnT[:, j % 2, c, :], w_sb[:, c, :],
                                                start=(c == 0), stop=(c == DC - 1))
                    last.then_inc(projected, 1)

            peeled(nc.tensor, NB // B1, project)
            pe.wait_ge(start_ready, 1)
            nc.tensor.matmul(ps_small[:, 0:NB], next_row[:], start[:, 0:NB], start=True, stop=False)
            nc.tensor.matmul(ps_small[:, 0:NB], wrap_row[:], start[:, 1:NB + 1], start=False, stop=True).then_inc(end_spread, 1)
            pe.wait_ge(classes_ready, 1)
            for t in range(NB):
                last = nc.tensor.matmul(ps_small[:, 64:65], classes[:, :, t], ones_b[:, 0:1], start=(t == 0), stop=(t == NB - 1))
            last.then_inc(counted, 1)
            pe.wait_ge(count_ready, 1)
            nc.tensor.matmul(ps_small[:, 66:67], upper_f[:], count[:], start=True, stop=True).then_inc(upto_ready, 1)
            pe.wait_ge(running_ready, 1)
            for t in range(NB):
                if t >= 2:
                    pe.wait_ge(rank_read, t - 1)
                o = ps_rank[t % 2][:, 0:KEYS]
                nc.tensor.matmul(o, count_b[:], upper_f[:], start=True, stop=False)
                if t > 0:
                    nc.tensor.matmul(o, ones_b[:], running[:, :, t - 1], start=False, stop=False)
                nc.tensor.matmul(o, upper[:], classes[:, :, t], start=False, stop=True).then_inc(ranked, 1)
            pe.wait_ge(passed_ready, 1)
            nc.tensor.matmul(ps_small[0:1, 128:128 + NB], ones_b[:, 0:1], passed[:], start=True, stop=True).then_inc(blocks_counted, 1)
            pe.wait_ge(max_ready, 1)
            nc.tensor.transpose(ps_tail[0:1, 0:P], deg_max[:], ident[:]).then_inc(max_turned, 1)


def attend(nc, outer, g):
    src_pad, table, records, xy = (g[k] for k in ("src_pad", "table", "records", "xy"))
    queue_in, queue_out = g["queue_in"], g["queue_out"]
    bias, gate_w, gate_b = (g[k] for k in ("bias", "gate_w", "gate_b"))
    ident, upper, ones_b, iota_x, iota_w, eps, plan, arena, bank = (
        g[k] for k in ("ident", "upper", "ones_b", "iota_x", "iota_w", "eps", "plan", "arena", "bank"))
    pick, share, rank, chosen, ids, slot = (g[k] for k in ("pick", "share", "rank", "chosen", "ids", "slot"))
    MOST_GROUPS = (E + GS - 1) // GS
    MOST_WINDOWS = (MOST_GROUPS + GW - 1) // GW
    MOST_BEFORE = E // GS + 2 * NB
    MOST_SLOTS = E + 2 * NB
    SLOTS_AFTER = PART + 1
    POOL_STEPS = 3
    WINDOW_STEPS = 14
    BLOCK_STEPS = 10
    GATE_STEPS = 15

    with ExitStack() as ctx:
        def sb(name, shape, dt=F32):
            return ctx.enter_context(nc.sbuf_tensor(name, shape, dt))

        def sem(name):
            return ctx.enter_context(nc.semaphore(name))

        rows = [arena[:, i * W * TROW:(i + 1) * W * TROW].rearrange("p (s r) -> p s r", r=TROW) for i in range(2)]
        recb = sb("recb", [P, 2, RROW])
        zeros = sb("zeros", [P, D])
        starts = sb("starts", [P, NB], I32)
        win_at = sb("win_at", [P, 2], I32)
        win_was = sb("win_was", [P, 2], I32)
        win_next = sb("win_next", [P, 2], I32)
        shift = sb("shift", [P, 2], I32)
        nbr = sb("nbr", [P, 2, W], I32)
        logit = sb("logit", [P, W, H])
        prob = sb("prob", [P, W, H])
        mask = sb("mask", [P, W])
        left = sb("left", [P, 1])
        top = sb("top", [P, H])
        top_new = sb("top_new", [P, H])
        drop = sb("drop", [P, H])
        fade = sb("fade", [P, H])
        denom = sb("denom", [P, H])
        dsum = sb("dsum", [P, H])
        acc = sb("acc", [P, D])
        bias_b = sb("bias_b", [P, D])
        gate_sb = sb("gate_sb", [P, DC, X])
        gate_bb = sb("gate_bb", [P, X])
        xy_out = sb("xy_out", [P, 2, 2 * D])
        total = sb("total", [P, 1])
        neg_mean = sb("neg_mean", [P, 1])
        square = sb("square", [P, D])
        sq_sum = sb("sq_sum", [P, 1])
        std = sb("std2", [P, 1])
        rstd = sb("rstd2", [P, 1])
        yT = sb("yT", [P, DC, P])
        score = sb("score", [P, X])
        best = sb("best", [P, 8])
        best_i = sb("best_i", [P, 8], U32)
        best_f = sb("best_f", [P, TOP])
        gap = sb("gap2", [P, 1])
        ratio = sb("ratio", [P, 1])
        pick_now = sb("pick_now", [P, TOP, X])
        rank_now = sb("rank_now", [P, TOP])
        both = sb("both", [P, X], BF16)
        junk = sb("junk2", [P, TOP, X])

        part = {name: sb(f"part_{name}", shape, dt) for name, shape, dt in (
            ("row", [P, X], F32), ("length", [P, X], F32), ("blocks_i", [P, X], I32), ("blocks_f", [P, X], F32),
            ("ends", [P, X], F32), ("base", [P, X], F32), ("picked", [P, PART, X], F32), ("slot_f", [P, TOP, PART], F32))}
        y_ring = sb("y_ring", [P, YRING, D])

        part_steps = sem("part_steps")
        part_lengths = sem("part_lengths")
        part_slots = sem("part_slots")
        rows_cleared = sem("rows_cleared")
        y_loaded = [sem(f"y_loaded{i}") for i in range(YRING)]
        dispatched = [sem(f"dispatched{i}") for i in range(YRING)]
        consts = sem("consts")
        cleared = [sem(f"cleared{p}") for p in range(2)]
        pool_filled = sem("pool_filled")
        own_pool = [sem(f"own_pool{p}") for p in range(2)]
        starts_loaded = sem("starts_loaded")
        rec_loaded = [sem(f"rec_loaded{p}") for p in range(2)]
        nbr_loaded = [sem(f"nbr_loaded{p}") for p in range(2)]
        rows_gathered = [sem(f"rows_gathered{p}") for p in range(2)]
        weighted = [sem(f"weighted{p}") for p in range(2)]
        group_summed = [sem(f"group_summed{p}") for p in range(2)]
        summed = [sem(f"summed{p}") for p in range(2)]
        sum_taken = [sem(f"sum_taken{p}") for p in range(2)]
        logits_ready = [sem(f"logits_ready{p}") for p in range(2)]
        probs_ready = [sem(f"probs_ready{p}") for p in range(2)]
        win_steps = [sem(f"win_steps{p}") for p in range(2)]
        blk_steps = sem("blk_steps")
        gate_steps = sem("gate_steps")
        mean_ready = sem("mean_ready")
        squared = sem("squared")
        std_ready = sem("std_ready2")
        y_ready = sem("y_ready")
        y_turned = sem("y_turned")
        yT_ready = sem("yT_ready")
        scored = sem("scored")
        gap_ready = sem("gap_ready")
        ratio_ready = sem("ratio_ready")
        both_ready = sem("both_ready")
        queued = sem("queued")
        xy_stored = [sem(f"xy_stored{p}") for p in range(2)]

        ps_sum = [bank[0], bank[1]]
        ps_y = bank[2]
        ps_gate = bank[3]
        ps_rank = bank[4]
        ps_part = bank[5]

        def chosen_of(eng, b):
            part = int(b >= PART) if isinstance(b, int) else eng.snap(b > PART - 1, min_val=0, max_val=1)
            return chosen[:, bass.ds(part, 1), :].rearrange("p o x -> p (o x)")

        def entry(eng, q, b, high):
            return eng.value_load(plan[0:1, q, bass.ds(b, 1)], min_val=1, max_val=high)

        def slots_of(eng, b):
            return entry(eng, 0, b, MOST_SLOTS)

        def groups_for(eng, slots):
            return eng.snap((slots + (GS - 1)) >> (GS.bit_length() - 1), min_val=1, max_val=MOST_GROUPS)

        def windows_for(eng, slots):
            return eng.snap((slots + (W - 1)) >> (W.bit_length() - 1), min_val=1, max_val=MOST_WINDOWS)

        def before(eng, q, b, high):
            return 0 if isinstance(b, int) and b < 2 else entry(eng, q, b, high)

        def groups_before_of(eng, b):
            return before(eng, 1, b, MOST_BEFORE)

        def windows_before_of(eng, b):
            return before(eng, 2, b, MOST_BEFORE)

        def slots_before_of(eng, b):
            return before(eng, 3, b, MOST_SLOTS)

        def part_in(eng, total, w, size):
            rest = eng.snap(total - w * size)
            return eng.snap((rest - (rest > size) * (rest - size)) & (2 * size - 1), min_val=1, max_val=size)

        block = ctx.enter_context(nc.Block())

        @block.sync
        def _(sp):
            with nc.allow_non_contiguous_dma(reason="one word of each record"):
                sp.dma_start(starts[:].unsqueeze(2), records[:, C_START:C_START + 1].bitcast(I32).rearrange("(b p) o -> p b o", p=P)
                             ).then_inc(starts_loaded, 16)
            sp.dma_start(bias_b[:], bias.rearrange("(o d) -> o d", o=1).partition_broadcast(P)).then_inc(consts, 16)
            sp.dma_start(gate_bb[:], gate_b.rearrange("(o d) -> o d", o=1).partition_broadcast(P)).then_inc(consts, 16)
            sp.dma_start(gate_sb[:], gate_w.rearrange("(c p) x -> p c x", p=P)).then_inc(consts, 16)

            def load(b, p, k):
                after(sp, y_ready, b - 1)
                sp.dma_start(recb[:, p, :], records[bass.ds(b * P, P), :]).then_inc(rec_loaded[p], 16)
                if not (isinstance(b, int) and b < 2):
                    sp.wait_ge(cleared[p], k * 32)
                    nc.sync.sem_inc(rows_cleared, 1)
                sp.dma_start(queue_in[bass.ds(b * (CLEAR * P), CLEAR * P), :].rearrange("(p r) d -> p r d", p=P),
                             zeros[:].unsqueeze(1).to_broadcast([P, CLEAR, D])).then_inc(cleared[p], 16)
                sp.dma_start(queue_out[bass.ds(b * (CLEAR_OUT * P) + LEAST_0 * P, CLEAR_OUT * P), :].rearrange("(p r) d -> p r d", p=P),
                             zeros[:].unsqueeze(1).to_broadcast([P, CLEAR_OUT, D])).then_inc(cleared[p], 16)
                if not (isinstance(b, int) and b < 2):
                    sp.dma_start(xy[bass.ds(b * P - 2 * P, P), :], xy_out[:, p, :]).then_inc(xy_stored[p], 16)

            sp.wait_ge(pool_filled, 4)
            alternating(sp, NB, load)
            for p in range(2):
                sp.wait_ge(cleared[p], 32 * ((NB + 1 - p) // 2))
            for p in range(2):
                sp.wait_ge(xy_stored[p], 16 * ((NB - 1 - p) // 2))

            def store_last(b):
                sp.wait_ge(y_ready, b + 1)
                sp.dma_start(xy[b * P:(b + 1) * P, :], xy_out[:, b % 2, :]).then_inc(xy_stored[b % 2], 16)

            for b in range(PART):
                if b >= YRING:
                    sp.wait_ge(dispatched[b % YRING], 16 * TOP * (b // YRING))
                sp.dma_start(y_ring[:, b % YRING, :], xy[b * P:(b + 1) * P, D:2 * D]).then_inc(y_loaded[b % YRING], 16)
                if b == PART * 2 // 3:
                    store_last(NB - 2)
            store_last(NB - 1)
            for p in range(2):
                sp.wait_ge(xy_stored[p], 16 * ((NB + 1 - p) // 2))

        @block.gpsimd
        def _(pool):
            def fetch_nbrs(p, steps, b):
                at = win_next[:, p:p + 1] if b is None else starts[:, bass.ds(b, 1)]
                steps.settle()
                steps.do(nc.gpsimd.tensor_tensor(win_at[:, p:p + 1], at, shift[:, 0:1], ALU.add))
                steps.settle()
                steps.do(nc.gpsimd.tensor_tensor(win_was[:, p:p + 1], win_at[:, p:p + 1], shift[:, 0:1], ALU.add))
                nc.gpsimd.indirect_dma_start(nbr[:, p, :], None, src_pad[:, :],
                                             bass.IndirectOffsetOnAxis(ap=win_at[:, p:p + 1], axis=0),
                                             bounds_check=E, oob_is_err=False).then_inc(nbr_loaded[p], 16)

            pool.wait_ge(blk_steps, 2)
            nc.gpsimd.memset(shift[:, 0:1], 0).then_inc(pool_filled, 1)
            nc.gpsimd.memset(shift[:, 1:2], W).then_inc(pool_filled, 1)
            nc.gpsimd.memset(nbr[:, :, :], 0).then_inc(pool_filled, 1)
            nc.gpsimd.memset(zeros[:], 0.0).then_inc(pool_filled, 1)
            pool.wait_ge(pool_filled, 4)
            pool.wait_ge(starts_loaded, 16)
            fetch_nbrs(0, Steps(pool, own_pool[0]), 0)

            def gather(b, p, k):
                slots = slots_of(pool, b)
                windows_before, slots_before = windows_before_of(pool, b), slots_before_of(pool, b)
                windows = windows_for(pool, slots)
                with nc.gpsimd.Fori(0, windows) as w:
                    with nc.gpsimd.If(w > 0):
                        pool.wait_ge(rows_gathered[p], (w * W + slots_before) * 16)
                        fetch_nbrs(p, Steps(pool, own_pool[p], (w + windows_before) * POOL_STEPS), None)
                    pool.wait_ge(nbr_loaded[p], (w + windows_before + 1) * 16)
                    pool.wait_ge(summed[p], w + windows_before + 1)
                    nc.gpsimd.tensor_tensor(win_next[:, p:p + 1], win_at[:, p:p + 1], shift[:, 1:2], ALU.add
                                            ).then_inc(own_pool[p], 1)
                    rest = pool.snap(slots - w * W)

                    def slot(s):
                        nc.gpsimd.indirect_dma_start(rows[p][:, s, :], None, table[:, :],
                                                     bass.IndirectOffsetOnAxis(ap=nbr[:, p, s:s + 1], axis=0)
                                                     ).then_inc(rows_gathered[p], 16)

                    slot(0)
                    for s in range(1, W):
                        if s == GS and not (isinstance(b, int) and b == NB - 1):
                            with nc.gpsimd.If(w < 1):
                                q = 1 - p
                                if isinstance(b, int) and b == 0:
                                    fetch_nbrs(q, Steps(pool, own_pool[q]), 1)
                                else:
                                    slots_q = slots_before_of(pool, b + 1)
                                    windows_q = windows_before_of(pool, b + 1)
                                    pool.wait_ge(rows_gathered[q], slots_q * 16)
                                    fetch_nbrs(q, Steps(pool, own_pool[q], windows_q * POOL_STEPS), b + 1)
                        with nc.gpsimd.If(rest > s):
                            slot(s)

            alternating(nc.gpsimd, NB, gather)
            pool.wait_ge(part_slots, 1)
            pool.wait_ge(rows_cleared, (MOST_0 + CLEAR - 1) // CLEAR + 2)
            for b in range(PART):
                pool.wait_ge(y_loaded[b % YRING], 16 * (b // YRING + 1))
                for c in range(TOP):
                    nc.gpsimd.indirect_dma_start(queue_in[:, :], bass.IndirectOffsetOnAxis(ap=slot[:, c, b:b + 1], axis=0),
                                                 y_ring[:, b % YRING, :], None).then_inc(dispatched[b % YRING], 16)
            for i in range(YRING):
                pool.wait_ge(dispatched[i], 16 * TOP * ((PART + YRING - 1 - i) // YRING))

        @block.vector
        def _(dve):
            for p in range(2):
                nc.vector.memset(rows[p][:, :, D:TROW], 0.0).then_inc(blk_steps, 1)
            nc.vector.memset(chosen[:], 0.0).then_inc(blk_steps, 1)
            nc.vector.memset(part["row"][:], 1.0).then_inc(part_steps, 1)
            dve.wait_ge(blk_steps, 3)
            for p in range(2):
                nc.vector.sem_inc(sum_taken[p], 1)
            dve.wait_ge(consts, 48)

            def gate_pick(b):
                steps = Steps(dve, gate_steps, b * GATE_STEPS)
                dve.wait_ge(scored, b + 1)
                steps.do(nc.vector.tensor_tensor(score[:], ps_gate[:, 0:X], gate_bb[:], ALU.add))
                steps.settle()
                steps.do(nc.vector.tensor_copy(rank_now[:], score[:, 0:TOP]))
                steps.do(nc.vector.max(best[:], score[:]))
                steps.settle()
                nc.vector.tensor_tensor(gap[:], best[:, 1:2], best[:, 0:1], ALU.subtract).then_inc(gap_ready, 1)
                steps.do(nc.vector.max_index(best_i[:], best[:], score[:]))
                steps.settle()
                steps.do(nc.vector.tensor_copy(best_f[:], best_i[:, 0:TOP]))
                steps.settle()
                for c in range(TOP):
                    steps.do(nc.vector.tensor_scalar(pick_now[:, c, :], iota_x[:], best_f[:, c:c + 1], None, ALU.is_equal))
                steps.settle()
                nc.vector.tensor_tensor(both[:], pick_now[:, 0, :], pick_now[:, 1, :], ALU.add).then_inc(both_ready, 1)
                steps.do(nc.vector.tensor_copy(pick[:, :, bass.ds(b, 1), :].rearrange("p c o x -> p c (o x)"), pick_now[:]))
                dve.wait_ge(ratio_ready, b + 1)
                steps.do(nc.vector.tensor_scalar(gap[:], ratio[:], 1.0, None, ALU.add))
                steps.settle()
                steps.do(nc.vector.reciprocal(share[:, bass.ds(b, 1), 0:1].rearrange("p o x -> p (o x)"), gap[:]))
                steps.settle()
                steps.do(nc.vector.tensor_tensor(share[:, bass.ds(b, 1), 1:2].rearrange("p o x -> p (o x)"), ratio[:],
                                                 share[:, bass.ds(b, 1), 0:1].rearrange("p o x -> p (o x)"), ALU.mult))
                return steps

            def gate_rank(b, steps):
                so_far = chosen_of(dve, b)
                dve.wait_ge(queued, b + 1)
                for c in range(TOP):
                    steps.do(nc.vector.tensor_tensor_reduce(
                        junk[:, c, :], ps_rank[:, 0:X], pick_now[:, c, :], 1.0, 0.0, ALU.mult, ALU.add, rank_now[:, c:c + 1]))
                steps.do(nc.vector.tensor_tensor(so_far, so_far, both[:], ALU.add))
                steps.settle()
                steps.do(nc.vector.tensor_copy(rank[:, bass.ds(b, 1), :].rearrange("p o x -> p (o x)"), rank_now[:]))
                steps.settle()
                assert steps.n == GATE_STEPS, steps.n

            def attend_block(b, p, k):
                slots = slots_of(dve, b)
                windows_before, slots_before = windows_before_of(dve, b), slots_before_of(dve, b)
                windows, groups = windows_for(dve, slots), groups_for(dve, slots)
                blk = Steps(dve, blk_steps, b * BLOCK_STEPS + 3)
                gate = None
                dve.wait_ge(rec_loaded[p], 16 * (k + 1))
                blk.do(nc.vector.memset(top[:], NEG))
                blk.do(nc.vector.memset(denom[:], 0.0))
                blk.do(nc.vector.memset(acc[:], 0.0))
                blk.do(nc.vector.tensor_copy(left[:], recb[:, p, C_DEG:C_DEG + 1]))
                with nc.vector.Fori(0, windows) as w:
                    n = part_in(dve, groups, w, GW)
                    seen = dve.snap(w + windows_before)
                    win = Steps(dve, win_steps[p], seen * WINDOW_STEPS)
                    blk.settle()
                    dve.wait_ge(rows_gathered[p], (part_in(dve, slots, w, W) + w * W + slots_before) * 16)
                    win.do(nc.vector.tensor_tensor(logit[:], rows[p][:, :, D:TROW],
                                                   recb[:, p, C_ADST:C_ADST + H].unsqueeze(1).to_broadcast([P, W, H]), ALU.add))
                    win.do(nc.vector.tensor_scalar(mask[:], iota_w[:], left[:, 0:1], MASK, ALU.is_ge, ALU.mult))
                    win.settle()
                    win.do(nc.vector.scalar_tensor_tensor(out=logit[:], in0=logit[:], scalar=SLOPE, in1=logit[:],
                                                          op0=ALU.mult, op1=ALU.max))
                    win.settle()
                    win.do(nc.vector.tensor_tensor(logit[:], logit[:], mask[:].unsqueeze(2).to_broadcast([P, W, H]), ALU.add))
                    win.settle()
                    win.do(nc.vector.tensor_reduce(top_new[:], logit[:].rearrange("p s h -> p h s"), AX.X, ALU.max))
                    win.settle()
                    win.do(nc.vector.tensor_tensor(top_new[:], top_new[:], top[:], ALU.max))
                    win.settle()
                    nc.vector.tensor_tensor(drop[:], top[:], top_new[:], ALU.subtract).then_inc(logits_ready[p], 1)
                    nc.vector.tensor_tensor(logit[:], logit[:], top_new[:].unsqueeze(1).to_broadcast([P, W, H]),
                                            ALU.subtract).then_inc(logits_ready[p], 1)
                    win.do(nc.vector.tensor_scalar(left[:], left[:], float(-W), None, ALU.add))
                    dve.wait_ge(logits_ready[p], (seen + 1) * 2)
                    win.do(nc.vector.tensor_copy(top[:], top_new[:]))
                    dve.wait_ge(probs_ready[p], (seen + 1) * 2)
                    win.do(nc.vector.tensor_reduce(dsum[:], prob[:].rearrange("p s h -> p h s"), AX.X, ALU.add))
                    win.do(nc.vector.tensor_tensor(denom[:], denom[:], fade[:], ALU.mult))
                    win.do(nc.vector.tensor_tensor(acc[:].rearrange("p (h d) -> p h d", h=H), acc[:].rearrange("p (h d) -> p h d", h=H),
                                                   fade[:].unsqueeze(2).to_broadcast([P, H, HD]), ALU.mult))
                    win.settle()
                    win.do(nc.vector.tensor_tensor(denom[:], denom[:], dsum[:], ALU.add))
                    with nc.vector.Fori(0, n) as i:
                        i = i.with_bounds(min_val=0, max_val=GW - 1)
                        slots = rows[p][:, bass.ds(i * GS, GS), 0:D].rearrange("p s (h d) -> p s h d", h=H)
                        nc.vector.tensor_tensor(slots, slots, prob[:, bass.ds(i * GS, GS), :].unsqueeze(3).to_broadcast([P, GS, H, HD]),
                                                ALU.mult).then_inc(weighted[p], 1)
                    if not (isinstance(b, int) and b == 0):
                        with nc.vector.If(w < 1):
                            gate = gate_pick(b - 1)
                    dve.wait_ge(summed[p], seen + 2)
                    win.do(nc.vector.tensor_tensor(acc[:], acc[:], ps_sum[p][:, 0:D], ALU.add))
                    win.settle()
                    win.do(nc.vector.tensor_tensor(acc[:], acc[:], ps_sum[p][:, D:2 * D], ALU.add))
                    win.settle()
                    assert win.n == WINDOW_STEPS, win.n
                    nc.vector.sem_inc(sum_taken[p], 1)
                blk.do(nc.vector.tensor_scalar(denom[:], denom[:], 1e-16, None, ALU.add))
                blk.settle()
                blk.do(nc.vector.reciprocal(denom[:], denom[:]))
                blk.settle()
                a3 = acc[:].rearrange("p (h d) -> p h d", h=H)
                blk.do(nc.vector.tensor_tensor(a3, a3, denom[:].unsqueeze(2).to_broadcast([P, H, HD]), ALU.mult))
                blk.settle()
                blk.do(nc.vector.tensor_tensor(acc[:], acc[:], bias_b[:], ALU.add))
                blk.settle()
                after(dve, xy_stored[p], 16 * k)
                blk.do(nc.vector.scalar_tensor_tensor(out=xy_out[:, p, 0:D], in0=acc[:], scalar=0.0, in1=recb[:, p, 0:D],
                                                      op0=ALU.max, op1=ALU.add, accum_out=total[:]))
                blk.settle()
                nc.vector.tensor_scalar(neg_mean[:], total[:], -1.0 / D, None, ALU.mult).then_inc(mean_ready, 1)
                nc.vector.tensor_copy(ids[:, bass.ds(b, 1)], recb[:, p, C_ID:C_ID + 1]).then_inc(mean_ready, 1)
                if gate is not None:
                    gate_rank(b - 1, gate)
                dve.wait_ge(std_ready, b + 1)
                blk.do(nc.vector.reciprocal(rstd[:], std[:]))
                blk.settle()
                nc.vector.tensor_scalar(xy_out[:, p, D:2 * D], xy_out[:, p, 0:D], neg_mean[:, 0:1], rstd[:, 0:1],
                                        ALU.add, ALU.mult).then_inc(y_ready, 1)
                if p == SLOTS_AFTER % 2 and not isinstance(b, int):
                    with nc.vector.If(k == SLOTS_AFTER // 2):
                        nc.vector.sem_inc(part_steps, 1)
                        dve.wait_ge(part_lengths, 1)
                        find_slots(nc, Steps(dve, part_steps, 2), ps_part[:, 0:X], 0.0, pick, rank, 0, PART, slot=slot, **part
                                   ).then_inc(part_slots, 1)
                dve.wait_ge(y_ready, b + 1)
                assert blk.n == BLOCK_STEPS, blk.n

            alternating(nc.vector, NB, attend_block)
            gate_rank(NB - 1, gate_pick(NB - 1))

        @block.scalar
        def _(act):
            def gate(b):
                act.wait_ge(y_turned, b + 1)
                nc.scalar.copy(yT[:].rearrange("p c n -> p (c n)"), ps_y[:, 0:D]).then_inc(yT_ready, 1)

            def gate_exp(b):
                act.wait_ge(gap_ready, b + 1)
                nc.scalar.activation(ratio[:], gap[:], ACT.Exp).then_inc(ratio_ready, 1)

            def exps(b, p, k):
                if not (isinstance(b, int) and b == 0):
                    gate(b - 1)
                windows, windows_before = windows_for(act, slots_of(act, b)), windows_before_of(act, b)
                with nc.scalar.Fori(0, windows) as w:
                    seen = act.snap(w + windows_before)
                    act.wait_ge(logits_ready[p], (seen + 1) * 2)
                    nc.scalar.activation(fade[:], drop[:], ACT.Exp).then_inc(probs_ready[p], 1)
                    nc.scalar.activation(prob[:], logit[:], ACT.Exp).then_inc(probs_ready[p], 1)
                    if not (isinstance(b, int) and b == 0):
                        with nc.scalar.If(w < 1):
                            gate_exp(b - 1)
                act.wait_ge(mean_ready, (b + 1) * 2)
                nc.scalar.activation(square[:], xy_out[:, p, 0:D], ACT.Square, bias=neg_mean[:, 0:1],
                                     accum_out=sq_sum[:]).then_inc(squared, 1)
                act.wait_ge(squared, b + 1)
                nc.scalar.activation(std[:], sq_sum[:], ACT.Sqrt, bias=eps[:, 0:1], scale=1.0 / D).then_inc(std_ready, 1)

            alternating(nc.scalar, NB, exps)
            gate(NB - 1)
            gate_exp(NB - 1)

        @block.tensor
        def _(pe):
            for p in range(2):
                nc.tensor.sem_inc(summed[p], 1)
            pe.wait_ge(consts, 48)

            def gate(b, p):
                pe.wait_ge(y_ready, b + 1)
                for c in range(DC):
                    last = nc.tensor.transpose(ps_y[:, c * P:(c + 1) * P], xy_out[:, p, D + c * P:D + (c + 1) * P], ident[:])
                last.then_inc(y_turned, 1)
                pe.wait_ge(yT_ready, b + 1)
                for c in range(DC):
                    last = nc.tensor.matmul(ps_gate[:, 0:X], yT[:, c, :], gate_sb[:, c, :], start=(c == 0), stop=(c == DC - 1))
                last.then_inc(scored, 1)

            def places(b):
                so_far = chosen_of(pe, b)
                pe.wait_ge(both_ready, b + 1)
                nc.tensor.matmul(ps_rank[:, 0:X], upper[:], both[:], start=True, stop=False)
                nc.tensor.matmul(ps_rank[:, 0:X], ones_b[:], so_far, start=False, stop=True).then_inc(queued, 1)

            def sums(b, p, k):
                if not (isinstance(b, int) and b == 0):
                    gate(b - 1, 1 - p)
                slots = slots_of(pe, b)
                groups_before, windows_before = groups_before_of(pe, b), windows_before_of(pe, b)
                windows, groups = windows_for(pe, slots), groups_for(pe, slots)
                with nc.tensor.Fori(0, windows) as w:
                    n = part_in(pe, groups, w, GW)
                    g0 = pe.snap(w * GW + groups_before)
                    pe.wait_ge(sum_taken[p], w + windows_before + 1)

                    def group(i, start):
                        pe.wait_ge(weighted[p], g0 + i + 1)
                        for c in range(0, GS, 2):
                            last = nc.tensor.matmul(ps_sum[p][:, :].rearrange("p (s d) -> p s d", s=2), ident[:],
                                                    rows[p][:, bass.ds(i * GS + c, 2), 0:D],
                                                    start=(start and c == 0), stop=True, skip_group_check=True)
                        last.then_inc(group_summed[p], 1)

                    group(0, True)
                    with nc.tensor.If(n > 1):
                        with nc.tensor.Fori(1, n) as i:
                            group(i.with_bounds(min_val=1, max_val=GW - 1), False)
                    pe.wait_ge(group_summed[p], g0 + n)
                    nc.tensor.sem_inc(summed[p], 1)
                if not (isinstance(b, int) and b == 0):
                    places(b - 1)
                if p == SLOTS_AFTER % 2 and not isinstance(b, int):
                    with nc.tensor.If(k == SLOTS_AFTER // 2):
                        pe.wait_ge(part_steps, 2)
                        nc.tensor.matmul(ps_part[:, 0:X], ones_b[:], chosen[:, 0, :], start=True, stop=True).then_inc(part_lengths, 1)

            alternating(nc.tensor, NB, sums)
            gate(NB - 1, (NB - 1) % 2)
            places(NB - 1)


def find_slots(nc, steps, lengths, first, pick, rank, low, high, row, length, blocks_i, blocks_f, ends, base, picked, slot_f, slot):
    do = steps.do
    do(nc.vector.tensor_copy(length[:], lengths))
    steps.settle()
    do(nc.vector.tensor_scalar(blocks_i[:], length[:], float(P - 1), None, ALU.add))
    steps.settle()
    do(nc.vector.tensor_scalar(blocks_i[:], blocks_i[:], P.bit_length() - 1, None, ALU.arith_shift_right))
    steps.settle()
    do(nc.vector.tensor_copy(blocks_f[:], blocks_i[:]))
    steps.settle()
    do(nc.vector.tensor_tensor_scan(ends[:], row[:], blocks_f[:], first, ALU.mult, ALU.add))
    steps.settle()
    do(nc.vector.tensor_tensor(base[:], ends[:], blocks_f[:], ALU.subtract))
    steps.settle()
    do(nc.vector.tensor_scalar(base[:], base[:], float(P), None, ALU.mult))
    for c in range(TOP):
        steps.settle()
        do(nc.vector.tensor_tensor(picked[:, low:high, :], pick[:, c, low:high, :],
                                   base[:].unsqueeze(1).to_broadcast([P, high - low, X]), ALU.mult))
        steps.settle()
        do(nc.vector.tensor_reduce(slot_f[:, c, low:high], picked[:, low:high, :], AX.X, ALU.add))
        steps.settle()
        do(nc.vector.tensor_tensor(slot_f[:, c, low:high], slot_f[:, c, low:high], rank[:, low:high, c], ALU.add))
    steps.settle()
    return nc.vector.tensor_copy(slot[:, :, low:high], slot_f[:, :, low:high])


def experts(nc, outer, g):
    w1, b1, w2, b2, gamma, beta, out = (g[k] for k in ("w1", "b1", "w2", "b2", "gamma", "beta", "out"))
    xy, queue_in, queue_out = (g[k] for k in ("xy", "queue_in", "queue_out"))
    ident, ones_b, eps, arena, bank = (g[k] for k in ("ident", "ones_b", "eps", "arena", "bank"))
    pick, share, rank, chosen, ids, slot = (g[k] for k in ("pick", "share", "rank", "chosen", "ids", "slot"))
    LOAD = 4
    STAGES = 2
    STORE_LAG = STAGES + 2
    HEAD = STORE_LAG + 2
    RING = 4
    BESIDE = PART // RING * RING
    SETTLE = 6
    assert TOP * N - TOP * PART * P >= (SETTLE + BESIDE + 2) * P
    JOIN_STEPS = 2
    NORM_STEPS = 3

    with ExitStack() as ctx:
        def sb(name, shape, dt=F32):
            return ctx.enter_context(nc.sbuf_tensor(name, shape, dt))

        def sem(name):
            return ctx.enter_context(nc.semaphore(name))

        w1_sb = arena[:, 0:X * DC * F].rearrange("p (x c f) -> p x c f", x=X, c=DC)
        w2_sb = arena[:, X * DC * F:X * (DC * F + FC * D)].rearrange("p (x c d) -> p x c d", x=X, c=FC)
        b1_cols = sb("b1_cols", [P, X * FC])
        b1_rows = sb("b1_rows", [X * FC, P])
        b2_b = sb("b2_b", [P, X, D])
        gamma_b = sb("gamma_b", [P, D])
        beta_b = sb("beta_b", [P, D])
        iota_fb = sb("iota_fb", [1, CAP])
        row_x = sb("row_x", [P, 2 * X])
        length = sb("length", [P, 2 * X])
        blocks_i = sb("blocks_i", [P, 2 * X], I32)
        blocks_f = sb("blocks_f", [P, 2 * X])
        ends = sb("ends", [P, 2 * X])
        base = sb("base", [P, 2 * X])
        picked = sb("picked", [P, NB, X])
        owner_f = sb("owner_f", [1, 2, CAP])
        owner_i = sb("owner_i", [1, CAP], I32)
        owner = sb("owner", [1, CAP], I32)
        totals = sb("totals", [1, 3], I32)
        slot_f = sb("slot_f", [P, TOP, NB])
        rows_in = sb("rows_in", [P, 2, D])
        xT = sb("xT", [P, 2, DC, P])
        hT = sb("hT", [P, 2, FC, P])
        rows_out = sb("rows_out", [P, 2, D])
        taken = sb("taken", [P, RING, TOP, D])
        xy_in = sb("xy_in", [P, RING, 2 * D])
        w1_now = sb("w1_now", [P, 2, DC, F])
        joined = sb("joined", [P, RING, D])
        final = arena[:, X * (DC * F + FC * D):][:, 0:RING * D].rearrange("p (r d) -> p r d", r=RING)
        through = taken[0:1, :, :, :].rearrange("o r c d -> o (r c d)").bitcast(BF16)[:, 0:CAP * X].rearrange("o (j x) -> o j x", x=X)
        y_ring = final
        square = sb("square3", [P, D])
        total = sb("total3", [P, RING])
        neg_mean = sb("neg_mean3", [P, RING])
        sq_sum = sb("sq_sum3", [P, RING])
        std = sb("std3", [P, RING])
        rstd = sb("rstd3", [P, RING])

        small_loaded = sem("small_loaded")
        weights_loaded = [sem(f"weights_loaded{i}") for i in range(X // LOAD)]
        weights_ready = sem("weights_ready")
        iota_made = sem("iota_made")
        lengths_ready = sem("lengths_ready")
        b1_turned = sem("b1_turned")
        b1_ready = sem("b1_ready")
        plan_steps = sem("plan_steps")
        slots_ready = sem("slots_ready")
        owners_ready = sem("owners_ready")
        y_loaded = [sem(f"y_loaded_1_{i}") for i in range(YRING)]
        dispatched = [sem(f"dispatched_1_{i}") for i in range(YRING)]
        in_loaded = [sem(f"in_loaded{p}") for p in range(2)]
        x_turned = sem("x_turned")
        xT_ready = sem("xT_ready")
        w1_ready = sem("w1_ready")
        up_done = sem("up_done")
        hT_ready = sem("hT_ready")
        down_done = sem("down_done")
        out_ready = sem("out_ready")
        out_stored = [sem(f"out_stored{p}") for p in range(2)]
        part_stored = sem("part_stored")
        taken_loaded = [sem(f"taken_loaded{i}") for i in range(RING)]
        xy_loaded = [sem(f"xy_loaded{i}") for i in range(RING)]
        join_read = sem("join_read")
        join_steps = sem("join_steps")
        end_steps = sem("end_steps")
        mean_ready = sem("mean_ready3")
        squared = sem("squared3")
        std_ready = sem("std_ready3")
        final_ready = sem("final_ready")
        final_stored = [sem(f"final_stored{i}") for i in range(RING)]

        ps_x = [bank[0], bank[1]]
        ps_up = [bank[2], bank[3]]
        ps_down = [bank[4], bank[5]]

        def stepping(eng, step, part_1=None, part_0_out=None, beside=None):
            blocks = eng.value_load(totals[0:1, 0:1], min_val=LEAST, max_val=FB + 1)
            blocks_0 = eng.value_load(totals[0:1, 2:3], min_val=LEAST_0, max_val=MOST_0)

            def at(s):
                return eng.snap(s).with_bounds(min_val=HEAD, max_val=FB + STORE_LAG)

            for s in range(HEAD):
                step(s, s % 2, lambda lag: s >= lag)
            first = eng.snap(((blocks_0 - HEAD) & 126) + HEAD)
            end = eng.snap(((blocks - HEAD) & 126) + HEAD)
            with eng.Fori(HEAD, first, 2) as s0:
                for i in range(2):
                    step(at(s0 + i), i, lambda lag: True)
            if part_1:
                part_1()
            for i in range(SETTLE):
                step(at(first + i), i % 2, lambda lag: True)
            if part_0_out:
                part_0_out()
            for i in range(RING):
                step(at(first + (SETTLE + i)), i % 2, lambda lag: True)
                if beside:
                    beside(i, i, 0)
            with eng.Fori(1, BESIDE // RING) as k:
                for i in range(RING):
                    step(at(first + (SETTLE + i) + k * RING), i % 2, lambda lag: True)
                    if beside:
                        beside(k * RING + i, i, k)
            with eng.Fori(eng.snap(first + (SETTLE + BESIDE)), end, 2) as s0:
                for i in range(2):
                    step(at(s0 + i), i, lambda lag: True)
            for i in range(STORE_LAG):
                step(at(end + i), i % 2, lambda lag: lag > i)

        def expert_of(eng, j):
            return eng.value_load(owner[0:1, bass.ds(j, 1)], min_val=0, max_val=X - 1)

        block = ctx.enter_context(nc.Block())

        @block.sync
        def _(sp):
            sp.dma_start(b1_rows[:], b1.rearrange("x (c p) -> (x c) p", p=P)).then_inc(small_loaded, 16)
            sp.dma_start(b2_b[:].rearrange("p x d -> p (x d)"),
                         b2.rearrange("(o x) d -> o (x d)", o=1).partition_broadcast(P)).then_inc(small_loaded, 16)
            sp.dma_start(gamma_b[:], gamma.rearrange("(o d) -> o d", o=1).partition_broadcast(P)).then_inc(small_loaded, 16)
            sp.dma_start(beta_b[:], beta.rearrange("(o d) -> o d", o=1).partition_broadcast(P)).then_inc(small_loaded, 16)
            sp.wait_ge(owners_ready, 1)

            def step(s, p, at_hand):
                if at_hand(0):
                    after(sp, x_turned, s - 1)
                    sp.dma_start(rows_in[:, p, :], queue_in[bass.ds(s * P, P), :]).then_inc(in_loaded[p], 16)

            def part_1():
                for i in range(YRING):
                    sp.wait_ge(dispatched[i], 16 * TOP * ((NB - PART + YRING - 1 - i) // YRING))

            def load_xy(b, p):
                after(sp, final_ready, 0 if isinstance(b, int) and b < RING else b - RING + 2)
                sp.dma_start(xy_in[:, p, :], xy[bass.ds(b * P, P), :]).then_inc(xy_loaded[p], 16)

            AHEAD = RING - 2

            def first_xy():
                for b in range(AHEAD):
                    load_xy(b, b)

            stepping(nc.sync, step, part_1, first_xy, lambda i, p, k: load_xy(i + AHEAD, (p + AHEAD) % RING))
            for b in range(BESIDE + AHEAD, NB):
                load_xy(b, b % RING)

        @block.gpsimd
        def _(pool):
            nc.gpsimd.iota(iota_fb[:], [[1, CAP]], base=0, channel_multiplier=0, allow_small_or_imprecise_dtypes=True
                           ).then_inc(iota_made, 1)
            def load_y(i):
                b = PART + i
                if i >= YRING:
                    pool.wait_ge(dispatched[i % YRING], 16 * TOP * (i // YRING))
                nc.gpsimd.dma_start(y_ring[:, i % YRING, :], xy[b * P:(b + 1) * P, D:2 * D]).then_inc(y_loaded[i % YRING], 16)

            load_y(0)
            load_y(1)
            for i in range(NB - PART):
                if i + 2 < NB - PART:
                    load_y(i + 2)
                if i % LOAD == 0 and i < X:
                    pool.wait_ge(weights_loaded[i // LOAD], 32 * LOAD)
                    nc.gpsimd.sem_inc(weights_ready, LOAD)
                if i == 0:
                    pool.wait_ge(slots_ready, 1)
                pool.wait_ge(y_loaded[i % YRING], 16 * (i // YRING + 1))
                for c in range(TOP):
                    nc.gpsimd.indirect_dma_start(queue_in[:, :], bass.IndirectOffsetOnAxis(ap=slot[:, c, PART + i:PART + i + 1], axis=0),
                                                 y_ring[:, i % YRING, :], None).then_inc(dispatched[i % YRING], 16)

            def finish(b):
                pool.wait_ge(final_ready, b + 2)
                nc.gpsimd.indirect_dma_start(out[:, :], bass.IndirectOffsetOnAxis(ap=ids[:, b:b + 1], axis=0),
                                             final[:, b % RING, :], None, bounds_check=N - 1, oob_is_err=False
                                             ).then_inc(final_stored[b % RING], 16)

            AHEAD = RING - 1
            for b in range(NB):
                if b == 0 or b == PART:
                    pool.wait_ge(part_stored, 1 + (b == PART))
                if b >= RING:
                    pool.wait_ge(join_read, b - RING + 1)
                for c in range(TOP):
                    nc.gpsimd.indirect_dma_start(taken[:, b % RING, c, :], None, queue_out[:, :],
                                                 bass.IndirectOffsetOnAxis(ap=slot[:, c, b:b + 1], axis=0)
                                                 ).then_inc(taken_loaded[b % RING], 16)
                if b >= AHEAD:
                    finish(b - AHEAD)
            for b in range(NB - AHEAD, NB):
                finish(b)
            for i in range(RING):
                pool.wait_ge(final_stored[i], 16 * ((NB + RING - 1 - i) // RING))

        @block.vector
        def _(dve):
            steps = Steps(dve, plan_steps)
            steps.do(nc.vector.memset(row_x[:], 1.0))
            nc.vector.sem_inc(final_ready, 1)
            dve.wait_ge(lengths_ready, 1)
            steps.do(nc.vector.tensor_copy(length[:], ps_up[0][:, 0:2 * X]))
            steps.settle()
            steps.do(nc.vector.tensor_scalar(blocks_i[:], length[:], float(P - 1), None, ALU.add))
            steps.settle()
            steps.do(nc.vector.tensor_scalar(blocks_i[:], blocks_i[:], P.bit_length() - 1, None, ALU.arith_shift_right))
            steps.settle()
            steps.do(nc.vector.tensor_copy(blocks_f[:], blocks_i[:]))
            steps.settle()
            steps.do(nc.vector.tensor_tensor_scan(ends[:], row_x[:], blocks_f[:], 0.0, ALU.mult, ALU.add))
            steps.settle()
            steps.do(nc.vector.tensor_tensor(base[:], ends[:], blocks_f[:], ALU.subtract))
            steps.settle()
            steps.do(nc.vector.tensor_scalar(base[:], base[:], float(P), None, ALU.mult))
            steps.do(nc.vector.tensor_scalar(totals[:, 1:2], ends[0:1, 2 * X - 1:2 * X], 1.0, None, ALU.add))
            steps.do(nc.vector.tensor_copy(totals[:, 2:3], ends[0:1, X - 1:X]))
            steps.settle()
            steps.do(nc.vector.tensor_scalar(totals[:, 1:2], totals[:, 1:2], 1, None, ALU.arith_shift_right))
            steps.settle()
            steps.do(nc.vector.tensor_scalar(totals[:, 0:1], totals[:, 1:2], 2.0, None, ALU.mult))
            dve.wait_ge(iota_made, 1)
            for g in range(2):
                steps.settle()
                steps.do(nc.vector.tensor_tensor(through[:], iota_fb[:].unsqueeze(2).to_broadcast([1, CAP, X]),
                                                 ends[0:1, g * X:(g + 1) * X].unsqueeze(1).to_broadcast([1, CAP, X]), ALU.is_ge))
                steps.settle()
                steps.do(nc.vector.tensor_reduce(owner_f[:, g, :], through[:], AX.X, ALU.add))
            steps.settle()
            steps.do(nc.vector.tensor_tensor(owner_f[:, 0, :], owner_f[:, 0, :], owner_f[:, 1, :], ALU.add))
            steps.settle()
            steps.do(nc.vector.tensor_scalar(owner_i[:], owner_f[:, 0, :], float(2 * X - 1), None, ALU.min))
            steps.settle()
            nc.vector.tensor_scalar(owner[:], owner_i[:], X - 1, None, ALU.bitwise_and).then_inc(owners_ready, 1)
            dve.wait_ge(b1_turned, 1)
            nc.vector.tensor_copy(b1_cols[:], ps_x[0][:, 0:X * FC]).then_inc(b1_ready, 1)
            for c in range(TOP):
                steps.do(nc.vector.tensor_tensor(picked[:, PART:NB, :], pick[:, c, PART:NB, :],
                                                 base[:, X:2 * X].unsqueeze(1).to_broadcast([P, NB - PART, X]), ALU.mult))
                steps.settle()
                steps.do(nc.vector.tensor_reduce(slot_f[:, c, PART:NB], picked[:, PART:NB, :], AX.X, ALU.add))
                steps.settle()
                steps.do(nc.vector.tensor_tensor(slot_f[:, c, PART:NB], slot_f[:, c, PART:NB], rank[:, PART:NB, c], ALU.add))
                steps.settle()
            nc.vector.tensor_copy(slot[:, :, PART:NB], slot_f[:, :, PART:NB]).then_inc(slots_ready, 1)
            dve.wait_ge(owners_ready, 1)
            dve.wait_ge(small_loaded, 64)

            def step(s, p, at_hand):
                if at_hand(STAGES):
                    j = s - STAGES
                    e = expert_of(dve, j)
                    dve.wait_ge(down_done, j + 1)
                    if not (isinstance(j, int) and j < 2):
                        dve.wait_ge(out_stored[p], (j >> 1) * 16)
                    nc.vector.tensor_tensor(rows_out[:, p, :], ps_down[p][:, 0:D],
                                            b2_b[:, bass.ds(e, 1), :].rearrange("p o d -> p (o d)"), ALU.add).then_inc(out_ready, 1)

            def join(b, p, k):
                one = Steps(dve, join_steps, b * JOIN_STEPS)
                dve.wait_ge(taken_loaded[p], (k + 1) * 16 * TOP)
                dve.wait_ge(xy_loaded[p], (k + 1) * 16)
                one.do(nc.vector.scalar_tensor_tensor(out=joined[:, p, :], in0=taken[:, p, 0, :],
                                                      scalar=share[:, bass.ds(b, 1), 0:1].rearrange("p o c -> p (o c)"),
                                                      in1=xy_in[:, p, D:2 * D], op0=ALU.mult, op1=ALU.add))
                one.settle()
                one.do(nc.vector.scalar_tensor_tensor(out=joined[:, p, :], in0=taken[:, p, 1, :],
                                                      scalar=share[:, bass.ds(b, 1), 1:2].rearrange("p o c -> p (o c)"),
                                                      in1=joined[:, p, :], op0=ALU.mult, op1=ALU.add, accum_out=total[:, p:p + 1]))
                one.settle()
                nc.vector.sem_inc(join_read, 1)
                nc.vector.tensor_scalar(neg_mean[:, p:p + 1], total[:, p:p + 1], -1.0 / D, None, ALU.mult).then_inc(mean_ready, 1)

            def norm(b, p, k):
                two = Steps(dve, end_steps, b * NORM_STEPS)
                two.do(nc.vector.scalar_tensor_tensor(out=xy_in[:, p, D:2 * D], in0=joined[:, p, :], scalar=neg_mean[:, p:p + 1],
                                                      in1=gamma_b[:], op0=ALU.add, op1=ALU.mult))
                after(dve, final_stored[p], k * 16)
                two.do(nc.vector.tensor_tensor(final[:, p, :], xy_in[:, p, 0:D], beta_b[:], ALU.add))
                dve.wait_ge(std_ready, b + 1)
                two.do(nc.vector.reciprocal(rstd[:, p:p + 1], std[:, p:p + 1]))
                two.settle()
                nc.vector.scalar_tensor_tensor(out=final[:, p, :], in0=xy_in[:, p, D:2 * D], scalar=rstd[:, p:p + 1], in1=final[:, p, :],
                                               op0=ALU.mult, op1=ALU.add).then_inc(final_ready, 1)
                assert two.n == NORM_STEPS

            def both(b, p, k):
                if not (isinstance(b, int) and b == NB - 1):
                    join(b + 1, (p + 1) % RING, k + (p + 1) // RING)
                norm(b, p, k)

            def part_0_out():
                half = dve.snap(dve.value_load(totals[0:1, 2:3], min_val=LEAST_0, max_val=MOST_0) >> 1)
                for p in range(2):
                    dve.wait_ge(out_stored[p], (half + 1) * 16)
                nc.vector.sem_inc(part_stored, 1)
                join(0, 0, 0)

            stepping(nc.vector, step, part_0_out=part_0_out, beside=both)
            half = dve.value_load(totals[0:1, 1:2], min_val=LEAST // 2, max_val=FB // 2 + 1)
            for p in range(2):
                dve.wait_ge(out_stored[p], half * 16)
            nc.vector.sem_inc(part_stored, 1)
            for b in range(BESIDE, NB):
                both(b, b % RING, b // RING)

        @block.scalar
        def _(act):
            def load_weights(e):
                nc.scalar.dma_start(w1_sb[:, e, :, :], w1[e, :, :].rearrange("(c p) f -> p c f", p=P)).then_inc(weights_loaded[e // LOAD], 16)
                nc.scalar.dma_start(w2_sb[:, e, :, :], w2[e, :, :].rearrange("(c p) d -> p c d", p=P)).then_inc(weights_loaded[e // LOAD], 16)

            for e in range(LOAD):
                load_weights(e)
            LATER = (X - LOAD) // HEAD
            assert LOAD + LATER * HEAD == X
            act.wait_ge(b1_ready, 1)

            def step(s, p, at_hand):
                j = s
                if isinstance(s, int):
                    for e in range(LOAD + s * LATER, LOAD + (s + 1) * LATER):
                        load_weights(e)
                if at_hand(0):
                    e = expert_of(act, s)
                    act.wait_ge(weights_ready, e + 1)
                    after(act, up_done, s - 1)
                    nc.scalar.copy(w1_now[:, p, :, :], w1_sb[:, bass.ds(e, 1), :, :].rearrange("p o c f -> p (o c) f")
                                   ).then_inc(w1_ready, 1)
                    act.wait_ge(x_turned, j + 1)
                    after(act, up_done, j - 1)
                    nc.scalar.copy(xT[:, p, :, :].rearrange("p c n -> p (c n)"), ps_x[p][:, 0:D]).then_inc(xT_ready, 1)
                if at_hand(1):
                    j = s - 1
                    e = expert_of(act, j)
                    act.wait_ge(up_done, j + 1)
                    after(act, down_done, j - 1)
                    for c in range(FC):
                        last = nc.scalar.activation(hT[:, 1 - p, c, :], ps_up[1 - p][:, c * P:(c + 1) * P], ACT.Relu,
                                                    bias=b1_cols[:, bass.ds(e * FC + c, 1)])
                    last.then_inc(hT_ready, 1)
                if at_hand(STORE_LAG):
                    j = s - STORE_LAG
                    act.wait_ge(out_ready, j + 1)
                    nc.scalar.dma_start(queue_out[bass.ds(j * P, P), :], rows_out[:, p, :]).then_inc(out_stored[p], 16)

            act.wait_ge(owners_ready, 1)
            def spread(b, p, k):
                act.wait_ge(mean_ready, b + 1)
                nc.scalar.activation(square[:], joined[:, p, :], ACT.Square, bias=neg_mean[:, p:p + 1],
                                     accum_out=sq_sum[:, p:p + 1]).then_inc(squared, 1)
                act.wait_ge(squared, b + 1)
                nc.scalar.activation(std[:, p:p + 1], sq_sum[:, p:p + 1], ACT.Sqrt, bias=eps[:, 0:1], scale=1.0 / D
                                     ).then_inc(std_ready, 1)

            stepping(nc.scalar, step, beside=spread)
            for b in range(BESIDE, NB):
                spread(b, b % RING, b // RING)

        @block.tensor
        def _(pe):
            nc.tensor.matmul(ps_up[0][:, 0:2 * X], ones_b[:], chosen[:].rearrange("p g x -> p (g x)"),
                             start=True, stop=True).then_inc(lengths_ready, 1)
            pe.wait_ge(small_loaded, 64)
            nc.tensor.transpose(ps_x[0][:, 0:X * FC], b1_rows[:], ident[0:X * FC, 0:X * FC]).then_inc(b1_turned, 1)
            pe.wait_ge(b1_ready, 1)
            pe.wait_ge(owners_ready, 1)

            def step(s, p, at_hand):
                j = s
                if at_hand(0):
                    k = s // 2 if isinstance(s, int) else s >> 1
                    pe.wait_ge(in_loaded[p], (k + 1) * 16)
                    after(pe, xT_ready, j - 1)
                    for c in range(DC):
                        last = nc.tensor.transpose(ps_x[p][:, c * P:(c + 1) * P], rows_in[:, p, c * P:(c + 1) * P], ident[:])
                    last.then_inc(x_turned, 1)
                if at_hand(1):
                    j = s - 1
                    pe.wait_ge(xT_ready, j + 1)
                    pe.wait_ge(w1_ready, j + 1)
                    after(pe, hT_ready, j - 1)
                    for f in range(FC):
                        for c in range(DC):
                            last = nc.tensor.matmul(ps_up[1 - p][:, f * P:(f + 1) * P],
                                                    w1_now[:, 1 - p, c, f * P:(f + 1) * P],
                                                    xT[:, 1 - p, c, :], start=(c == 0), stop=(c == DC - 1))
                    last.then_inc(up_done, 1)
                if at_hand(STAGES):
                    j = s - STAGES
                    e = expert_of(pe, j)
                    pe.wait_ge(hT_ready, j + 1)
                    after(pe, out_ready, j - 1)
                    for c in range(FC):
                        last = nc.tensor.matmul(ps_down[p][:, 0:D], hT[:, p, c, :],
                                                w2_sb[:, bass.ds(e, 1), c, :].rearrange("p o d -> p (o d)"),
                                                start=(c == 0), stop=(c == FC - 1))
                    last.then_inc(down_done, 1)

            stepping(nc.tensor, step)


_INS = ["x", "src", "dst", "L0_gnn_W", "L0_gnn_att_src", "L0_gnn_att_dst", "L0_gnn_bias", "L0_ffn_gate_w", "L0_ffn_gate_b",
        "L0_ffn_w1", "L0_ffn_b1", "L0_ffn_w2", "L0_ffn_b2", "L0_ffn_gamma", "L0_ffn_beta"]


def kernel(**inputs):
    import numpy as _np
    import concourse.bacc as _bacc
    from concourse import mybir as _mybir
    from concourse.bass_utils import run_bass_kernel_spmd as _run

    nc = _bacc.Bacc("TRN2", target_bir_lowering=False, num_devices=1)
    arrays, args = {}, []
    for name in _INS:
        a = _np.ascontiguousarray(inputs[name])
        arrays[f"in_{name}_dram"] = a
        args.append(nc.dram_tensor(f"in_{name}_dram", a.shape, _mybir.dt.from_np(a.dtype), kind="ExternalInput").ap())
    args.append(nc.dram_tensor("out_0_dram", (N, D), _mybir.dt.float32, kind="ExternalOutput").ap())
    gnn_ffn_kernel(nc, *args)
    r = _run(nc, [arrays], core_ids=[0])
    return r.results[0]["out_0_dram"]
```
